# Optimizing a Trainium2 kernel written in Bass

```python
import numpy as np
import jax
import jax.numpy as jnp

def _softmax(x, axis=-1):
    return jax.nn.softmax(x, axis=axis)

def _gelu(x):
    return jax.nn.gelu(x, approximate=True)

def _silu(x):
    return jax.nn.silu(x)

def _sigmoid(x):
    return jax.nn.sigmoid(x)

def _layernorm(x, axis=-1, eps=1e-05):
    m = jnp.mean(x, axis=axis, keepdims=True)
    v = jnp.var(x, axis=axis, keepdims=True)
    return (x - m) / jnp.sqrt(v + eps)

def _scatter_add(tgt, idx, src, axis=0):
    return tgt.at[idx].add(src)

def _segment_sum(src, seg, n):
    return jax.ops.segment_sum(src, seg, n)
kernel_name = 'mk_prb_d1_jaxref_r8_12df89'

def setup_inputs(seed: int=0):
    np.random.seed(seed)
    _w = jnp.asarray

    def _L0_attn_setup():
        import jax, jax.numpy as jnp
        import numpy as np
        B, T, C = (64, 32, 128)
        N_HEAD, HEAD_SIZE, KV_RANK = (16, 64, 128)
        BLOCK_SIZE = 32
        key = jax.random.key(seed)
        ks = jax.random.split(key, 5)
        HD = N_HEAD * HEAD_SIZE

        def init(k, shape):
            fan_in = shape[0]
            bound = 1.0 / np.sqrt(fan_in)
            return jax.random.uniform(k, shape, jnp.float32, -bound, bound)
        return {'x': jax.random.normal(ks[0], (B, T, C), jnp.float32), 'w_kv_down': init(ks[1], (C, KV_RANK)), 'w_kv_up': init(ks[2], (KV_RANK, 2 * HD)), 'w_q': init(ks[3], (C, HD)), 'w_out': init(ks[4], (HD, C))}
    _L0_attn_in = _L0_attn_setup()

    def _L0_ffn_setup():
        import jax, jax.numpy as jnp
        import numpy as np
        B, T, D, E, H = (8, 256, 128, 8, 32)
        LN_EPS = 1e-05
        key = jax.random.key(seed)
        ks = jax.random.split(key, 4)
        return {'x': jax.random.normal(ks[0], (B, T, D), dtype=jnp.float32), 'Wg': jax.random.normal(ks[1], (E, D), dtype=jnp.float32) * 0.02, 'ln_scale': jnp.ones((E, D), dtype=jnp.float32), 'ln_bias': jnp.zeros((E, D), dtype=jnp.float32), 'W1': jax.random.normal(ks[2], (E, D, H), dtype=jnp.float32) * 0.02, 'b1': jnp.zeros((E, H), dtype=jnp.float32), 'W2': jax.random.normal(ks[3], (E, H, D), dtype=jnp.float32) * 0.02, 'b2': jnp.zeros((E, D), dtype=jnp.float32)}
    _L0_ffn_in = _L0_ffn_setup()
    _d = {'L0_attn_x': _L0_attn_in['x'], 'L0_attn_w_kv_down': _L0_attn_in['w_kv_down'], 'L0_attn_w_kv_up': _L0_attn_in['w_kv_up'], 'L0_attn_w_q': _L0_attn_in['w_q'], 'L0_attn_w_out': _L0_attn_in['w_out'], 'L0_ffn_Wg': _L0_ffn_in['Wg'], 'L0_ffn_ln_scale': _L0_ffn_in['ln_scale'], 'L0_ffn_ln_bias': _L0_ffn_in['ln_bias'], 'L0_ffn_W1': _L0_ffn_in['W1'], 'L0_ffn_b1': _L0_ffn_in['b1'], 'L0_ffn_W2': _L0_ffn_in['W2'], 'L0_ffn_b2': _L0_ffn_in['b2']}
    _x0 = _d['L0_attn_x']
    _d['L0_attn_x'] = jax.random.normal(jax.random.fold_in(jax.random.key(seed), 1), (4, 512, 128), dtype=_x0.dtype)
    del _x0
    return _d

def reference(L0_attn_x, L0_attn_w_kv_down, L0_attn_w_kv_up, L0_attn_w_q, L0_attn_w_out, L0_ffn_Wg, L0_ffn_ln_scale, L0_ffn_ln_bias, L0_ffn_W1, L0_ffn_b1, L0_ffn_W2, L0_ffn_b2):

    def _L0_attn_ref(x, w_kv_down, w_kv_up, w_q, w_out):
        import jax, jax.numpy as jnp
        import numpy as np
        B, T, C = (64, 32, 128)
        N_HEAD, HEAD_SIZE, KV_RANK = (16, 64, 128)
        BLOCK_SIZE = 32
        Bx, Tx, Cx = x.shape
        HD = N_HEAD * HEAD_SIZE
        latent_kv = x @ w_kv_down
        kv = latent_kv @ w_kv_up
        k, v = (kv[..., :HD], kv[..., HD:])
        k = k.reshape(Bx, Tx, N_HEAD, HEAD_SIZE)
        v = v.reshape(Bx, Tx, N_HEAD, HEAD_SIZE)
        q = (x @ w_q).reshape(Bx, Tx, N_HEAD, HEAD_SIZE)
        scale = HEAD_SIZE ** (-0.5)
        att = jnp.einsum('bqhd,bkhd->bhqk', q, k) * scale
        causal = jnp.tril(jnp.ones((Tx, Tx), dtype=bool))
        att = jnp.where(causal, att, -jnp.inf)
        att = jax.nn.softmax(att, axis=-1)
        y = jnp.einsum('bhqk,bkhd->bqhd', att, v)
        y = y.reshape(Bx, Tx, HD)
        return y @ w_out

    def _L0_ffn_ref(x, Wg, ln_scale, ln_bias, W1, b1, W2, b2):
        import jax, jax.numpy as jnp
        import numpy as np
        B, T, D, E, H = (8, 256, 128, 8, 32)
        LN_EPS = 1e-05
        Bs, Ts, Ds = x.shape
        xt = x.reshape(Bs * Ts, Ds)
        logits = xt @ Wg.T
        top1 = jnp.argmax(logits, axis=-1)
        mu = jnp.mean(xt, axis=-1, keepdims=True)
        var = jnp.mean(jnp.square(xt - mu), axis=-1, keepdims=True)
        xhat = (xt - mu) * jax.lax.rsqrt(var + LN_EPS)
        n_experts = Wg.shape[0]

        def body(y, p):
            s_e, b_e, w1, bb1, w2, bb2, eid = p
            h = jax.nn.gelu((xhat * s_e + b_e) @ w1 + bb1, approximate=False)
            out = h @ w2 + bb2
            mask = (top1 == eid)[:, None].astype(out.dtype)
            return (y + mask * out, None)
        y0 = jnp.zeros_like(xt)
        y, _ = jax.lax.scan(body, y0, (ln_scale, ln_bias, W1, b1, W2, b2, jnp.arange(n_experts)))
        return y.reshape(Bs, Ts, Ds)
    x = L0_attn_x
    xn = _layernorm(x, axis=-1)
    x = x + _L0_attn_ref(xn, L0_attn_w_kv_down, L0_attn_w_kv_up, L0_attn_w_q, L0_attn_w_out) + _L0_ffn_ref(xn, L0_ffn_Wg, L0_ffn_ln_scale, L0_ffn_ln_bias, L0_ffn_W1, L0_ffn_b1, L0_ffn_W2, L0_ffn_b2)
    return x

_drawn_inputs = setup_inputs


def setup_inputs(seed=0):
    import zlib

    import numpy as np

    out = dict(_drawn_inputs(seed))
    spreads = {'L0_ffn_ln_scale': (1.0, 0.6),
     'L0_ffn_ln_bias': (0.0, 0.8),
     'L0_ffn_b1': (0.0, 0.8),
     'L0_ffn_b2': (0.0, 0.1)}
    factors = {'L0_attn_w_q': 8.0, 'L0_ffn_W1': 4.001, 'L0_ffn_W2': 3.646}
    for name, (base, spread) in spreads.items():
        noise = np.random.default_rng([zlib.crc32(name.encode()), seed]).standard_normal(out[name].shape)
        drawn = base * np.exp(spread * noise) if base else spread * noise
        out[name] = jnp.asarray(drawn.astype(out[name].dtype))
    for name, factor in factors.items():
        out[name] = (out[name] * factor).astype(out[name].dtype)
    return out
```

```python
import concourse.bass as bass
from concourse import mybir
from contextlib import ExitStack

F32 = mybir.dt.float32
F32R = mybir.dt.float32r
BF16 = mybir.dt.bfloat16
ALU = mybir.AluOpType
ACT = mybir.ActivationFunctionType

P = 128
NEG = -1.0e30
LN_EPS = 1e-5


def attention_and_experts(nc, x, w_kv_down, w_kv_up, w_q, w_out, wg, ln_scale, ln_bias, w1, b1, w2, b2, out):
    B, T, C = x.shape
    HD = w_q.shape[1]
    E, _, HID = w1.shape
    DH = 64
    PAIRS = HD // P
    TT = T // P
    NT = B * TT
    TOK = B * T
    G = E * HID // P
    EG = E // G
    UNITS = PAIRS * B
    SCALE = float(DH) ** -0.5
    assert C == P and T == 512 and w_kv_down.shape[1] == P and B == 4

    with ExitStack() as ctx:
        def sb(name, shape, dt=F32):
            return ctx.enter_context(nc.sbuf_tensor(name, shape, dt))

        def bank(name):
            return ctx.enter_context(nc.psum_tensor(name, [P, 512], F32))

        def sem(name):
            return ctx.enter_context(nc.semaphore(name))

        yT = sb("yT", [P, PAIRS, TOK])
        xn = yT[:, 7, :].rearrange("p (t c) -> p t c", c=C)
        xhat = yT[:, 6, :].rearrange("p (t c) -> p t c", c=C)
        xnT = yT[:, 5, :]
        xhatT = yT[:, 4, :]
        kv_up = yT[:, 3, :]
        wq_raw = yT[:, 2, 0:HD]
        w1_sb, w1s, w1b = (yT[:, 2, HD + n * E * HID:HD + (n + 1) * E * HID].rearrange("p (e h) -> p e h", e=E)
                           for n in range(3))
        x_sb = yT[:, 1, :].rearrange("p (t c) -> p t c", c=C)
        mask_new = yT[0:E, 0, :]
        wd, wdT = yT[:, 2, TOK - 2 * P:TOK - P], yT[:, 2, TOK - P:TOK]
        xh = sb("xh", [P, TOK], F32R)
        xl = sb("xl", [P, TOK], F32R)
        w_all = sb("w_all", [P, PAIRS, 6, P], F32R)
        w_qk = sb("w_qk", [P, 4, P], F32R)
        w_v = sb("w_v", [P, 2, P], F32R)
        gT = sb("gT", [P, G, TOK])
        mask_kept = nc.dram_tensor("mask_kept", [E, TOK], F32).ap()
        w2_sb = sb("w2_sb", [P, G, C])
        b2_sb = sb("b2_sb", [E, C])
        rows8 = sb("rows8", [E, 3, C])
        cols8 = sb("cols8", [P, 3, E])
        b1_rows = sb("b1_rows", [G, P])
        bias_h = sb("bias_h", [P, G])
        ident = sb("ident", [P, P])
        neg_qk = sb("neg_qk", [P, 512])
        ones = sb("ones", [P, DH])
        ones_r = sb("ones_r", [P, P], F32R)
        expand = sb("expand", [E, E * HID])
        order = sb("order", [P, E])
        stats = sb("stats", [P, NT, 6])
        mv = sb("mv", [P, NT, 2])
        nrm = sb("nrm", [P, 4, NT])
        logit = sb("logit", [P, NT, E])
        pick = sb("pick", [P, NT, E])
        best = sb("best", [P, 2, NT])
        QSM = [[sb(f"QSM{i}{h}", [P, 2, 512], F32R) for h in range(2)] for i in range(2)]
        QS = [[q[:, 0, :] for q in row] for row in QSM]
        QM = [[q[:, 1, :] for q in row] for row in QSM]
        KD = [[sb(f"KD{i}{h}", [P, 512], F32R) for h in range(2)] for i in range(2)]
        KL = [[sb(f"KL{i}{h}", [P, 512], F32R) for h in range(2)] for i in range(2)]
        PR = [[sb(f"PR{i}{h}", [P, 1280]) for h in range(2)] for i in range(2)]
        PS = [[sb(f"PS{i}{h}", [P, 384]) for h in range(2)] for i in range(2)]
        VS = [sb(f"VS{i}", [P, 512]) for i in range(4)]
        DG = [sb(f"DG{h}", [P, TT, P], F32R) for h in range(2)]
        mx = [sb(f"mx{h}", [P, TT]) for h in range(2)]
        scratch = sb("scratch", [P, 512])
        rden = sb("rden", [P, 512])
        wout_sb = PR[0][1][:, 0:PAIRS * C].rearrange("p (r c) -> p r c", c=C)
        x_again = [PR[0][0][:, 0:512], PR[0][0][:, 512:1024], VS[2][:], VS[0][:]]
        res = [VS[1], scratch]
        maskT = xl[0:E, :].bitcast(F32)

        st_a, st_b, st_c = bank("st_a"), bank("st_b"), bank("st_c")
        bd, be = bank("bd"), bank("be")
        bq, bk = bank("bq"), bank("bk")
        by = bank("by")

        d_x = [sem(f"d_x{b}") for b in range(B)]
        d_wd = sem("d_wd")
        d_kv = sem("d_kv")
        d_wq = sem("d_wq")
        d_small = sem("d_small")
        d_late = sem("d_late")
        d_mask = sem("d_mask")
        d_xa = [sem(f"d_xa{b}") for b in range(B)]
        d_wqk = sem("d_wqk")
        d_wv = sem("d_wv")
        d_out = [sem(f"d_out{i}") for i in range(2)]
        g_const = sem("g_const")
        g_step = sem("g_step")
        v_step = sem("v_step")
        p_wdT = sem("p_wdT")
        v_wdT = sem("v_wdT")
        p_fold = sem("p_fold")
        a_fold = sem("a_fold")
        v_fold = sem("v_fold")
        v_var = sem("v_var")
        a_std = sem("a_std")
        v_xn = sem("v_xn")
        p_xnT = sem("p_xnT")
        a_xnT = sem("a_xnT")
        v_xnT = sem("v_xnT")
        v_xhat = sem("v_xhat")
        p_xhatT = sem("p_xhatT")
        v_xhatT = sem("v_xhatT")
        p_rows = sem("p_rows")
        v_cols = sem("v_cols")
        p_bias = sem("p_bias")
        v_bias = sem("v_bias")
        p_logit = sem("p_logit")
        v_mask = sem("v_mask")
        p_hid = sem("p_hid")
        a_hid = sem("a_hid")
        p_maskT = sem("p_maskT")
        v_maskT = sem("v_maskT")
        p_exp = sem("p_exp")
        v_gm = sem("v_gm")
        s_q, s_k, s_v = sem("s_q"), sem("s_k"), sem("s_v")
        a_q, a_k, a_v = sem("a_q"), sem("a_k"), sem("a_v")
        v_q, v_k = sem("v_q"), sem("v_k")
        s_x, v_x = sem("s_x"), sem("v_x")
        v_turn = sem("v_turn")
        g_d, s_m, a_m = sem("g_d"), sem("s_m"), sem("a_m")
        s_st, a_e = sem("s_st"), sem("a_e")
        g_turn = sem("g_turn")
        g_s1 = sem("g_s1")
        g_s = sem("g_s")
        s_y, s_l = sem("s_y"), sem("s_l")
        a_r, v_r, v_r2 = sem("a_r"), sem("v_r"), sem("v_r2")
        v_n = sem("v_n")
        s_o, v_o = sem("s_o"), sem("v_o")

        x_v = x.rearrange("b (j p) c -> p (b j) c", p=P)
        out_v = out.rearrange("b (j p) c -> p (b j) c", p=P)

        block = ctx.enter_context(nc.Block())

        tbank = [st_a, st_b, st_c, by]
        mbank = [bd, be, bq, bk]

        @block.sync
        def _(sp):
            sp.dma_start(wd, w_kv_down).then_inc(d_wd, 16)
            for b in range(B):
                sp.dma_start(x_sb[:, b * TT:(b + 1) * TT, :], x_v[:, b * TT:(b + 1) * TT, :]).then_inc(d_x[b], 16)
            sp.dma_start(kv_up, w_kv_up).then_inc(d_kv, 16)
            sp.dma_start(wq_raw, w_q).then_inc(d_wq, 16)
            sp.dma_start(rows8[:, 0, :], wg).then_inc(d_small, 16)
            sp.dma_start(rows8[:, 1, :], ln_scale).then_inc(d_small, 16)
            sp.dma_start(rows8[:, 2, :], ln_bias).then_inc(d_small, 16)
            sp.dma_start(b1_rows[:], b1.rearrange("(g e) h -> g (e h)", g=G)).then_inc(d_small, 16)
            sp.dma_start(w1_sb, w1.rearrange("e d h -> d e h")).then_inc(d_small, 16)
            sp.dma_start(w2_sb[:], w2.rearrange("(g e) h c -> (e h) g c", g=G)).then_inc(d_late, 16)
            sp.dma_start(b2_sb[:], b2).then_inc(d_late, 16)
            sp.wait_ge(v_maskT, B)
            sp.dma_start(mask_kept, mask_new).then_inc(d_mask, 16)
            sp.wait_ge(a_fold, 5)
            sp.wait_ge(v_fold, 5)
            sp.dma_start(w_qk[:].bitcast(F32), w_all[:, 0, 0:4, :].bitcast(F32)).then_inc(d_wqk, 16)
            sp.dma_start(w_v[:].bitcast(F32), w_all[:, 0, 4:6, :].bitcast(F32)).then_inc(d_wv, 16)
            sp.wait_ge(d_mask, 16)
            with sp.Fori(1, PAIRS) as p:
                sp.wait_ge(s_k, B * p)
                sp.dma_start(w_qk[:].bitcast(F32), w_all[:, p, 0:4, :].bitcast(F32)).then_inc(d_wqk, 16)
                sp.wait_ge(s_v, B * p)
                sp.dma_start(w_v[:].bitcast(F32), w_all[:, p, 4:6, :].bitcast(F32)).then_inc(d_wv, 16)
            sp.wait_ge(s_l, UNITS - 1)
            sp.wait_ge(s_y, UNITS - 1)
            sp.dma_start(wout_sb, w_out.rearrange("(r p) c -> p r c", p=P)).then_inc(d_late, 16)
            sp.dma_start(maskT, mask_kept).then_inc(d_late, 16)
            for b in range(B):
                sp.dma_start(x_again[b].rearrange("p (t c) -> p t c", c=C), x_v[:, b * TT:(b + 1) * TT, :]).then_inc(d_xa[b], 16)
            for b in range(B):
                sp.wait_ge(v_o, b + 1)
                sp.dma_start(out_v[:, b * TT:(b + 1) * TT, :],
                             res[b % 2][:].rearrange("p (t c) -> p t c", c=C)).then_inc(d_out[b % 2], 16)
            for i in range(2):
                sp.wait_ge(d_out[i], 16 * B // 2)

        @block.gpsimd
        def _(pool):
            done = [0]

            def ordered(ins):
                done[0] += 1
                ins.then_inc(g_step, 1)
                pool.wait_ge(g_step, done[0])

            ordered(nc.gpsimd.memset(ident[:], 0.0))
            nc.gpsimd.affine_select(out=ident[:], in_=ident[:], compare_op=ALU.not_equal, fill=1.0, base=0,
                                    pattern=[[-1, P]], channel_multiplier=1).then_inc(g_const, 1)
            ordered(nc.gpsimd.memset(neg_qk[:], 0.0))
            nc.gpsimd.affine_select(out=neg_qk[:, 384:512], in_=neg_qk[:, 384:512], compare_op=ALU.is_ge,
                                    fill=NEG, base=0, pattern=[[-1, P]], channel_multiplier=1).then_inc(g_const, 1)
            ordered(nc.gpsimd.memset(expand[:], 0.0))
            nc.gpsimd.affine_select(out=expand[:].rearrange("e (f h) -> e f h", f=E),
                                    in_=expand[:].rearrange("e (f h) -> e f h", f=E),
                                    compare_op=ALU.not_equal, fill=1.0, base=0,
                                    pattern=[[-1, E], [0, HID]], channel_multiplier=1).then_inc(g_const, 1)
            nc.gpsimd.memset(ones[:], 1.0)
            nc.gpsimd.memset(ones_r[:].bitcast(F32), 1.0)
            for e in range(E):
                last = nc.gpsimd.memset(order[:, e:e + 1], float(E - e))
            ordered(last)
            for i in range(2):
                ordered(nc.gpsimd.memset(KL[i][0][DH:P, :].bitcast(F32), -1.0 / DH))
                last = nc.gpsimd.memset(KL[i][1][0:DH, :].bitcast(F32), -1.0 / DH)
                if i == 0:
                    ordered(last)
            last.then_inc(g_const, 1)
            pool.wait_ge(g_const, 4)

            nsum = [0]

            def diagonal(u, h):
                pool.wait_ge(v_x, 3 * (2 * u + h + 1))
                nc.gpsimd.tensor_tensor(DG[h][:], ident[:].unsqueeze(1).to_broadcast([P, TT, P]),
                                        mx[h][:].unsqueeze(2).to_broadcast([P, TT, P]),
                                        ALU.mult).then_inc(g_d, 1)

            def sums(u, i, h):
                pr, ps = PR[i][h], PS[i][h]
                pool.wait_ge(a_e, 3 * (2 * u + h + 1))
                pool.sem_inc(g_turn, 1)
                base = 4 * (2 * u + h)
                for blocks in (pr[:, 0:1024].rearrange("p (k c) -> p k c", k=2)[:, :, 0:P],
                               pr[:, 896:1152].rearrange("p (k c) -> p k c", k=2)):
                    nc.gpsimd.affine_select(out=blocks, in_=blocks, compare_op=ALU.is_ge, fill=0.0, base=0,
                                            pattern=[[0, 2], [1, P]], channel_multiplier=-1).then_inc(g_s1, 1)
                pool.wait_ge(g_s1, base + 2)
                nc.gpsimd.tensor_tensor(ps[:, 0:384], pr[:, 128:512], pr[:, 512:896], ALU.add).then_inc(g_s1, 1)
                pool.wait_ge(g_s1, base + 3)
                nc.gpsimd.tensor_tensor(ps[:, 128:384], ps[:, 128:384], pr[:, 1024:1280], ALU.add).then_inc(g_s1, 1)
                pool.wait_ge(g_s1, base + 4)
                nc.gpsimd.tensor_tensor(ps[:, 256:384], ps[:, 256:384], pr[:, 896:1024], ALU.add).then_inc(g_s, 1)

            def step(u, i, first=False, more=True):
                if not first:
                    sums(u, i, 0)
                    sums(u, i, 1)
                if more:
                    diagonal(u + 1, 0)
                    diagonal(u + 1, 1)

            step(-1, 1, first=True)
            for b in range(B):
                step(b, b % 2)
            with pool.Fori(1, PAIRS - 1) as p:
                for b in range(B):
                    step(B * p + b, b % 2)
            for b in range(B):
                step(B * (PAIRS - 1) + b, b % 2, more=b < B - 1)

        @block.scalar
        def _(act):
            for n in range(4):
                act.wait_ge(p_fold, n + 1)
                o = (2, 4)[n // 2]
                dst = w_all[:, 4 * (n % 2):4 * (n % 2) + 4, o, :]
                nc.scalar.activation(dst, mbank[n][:].rearrange("p (r c) -> p r c", c=P), ACT.Copy).then_inc(a_fold, 1)
            act.wait_ge(d_wq, 16)
            nc.scalar.activation(w_all[:, :, 0, :], wq_raw.rearrange("p (r c) -> p r c", c=P), ACT.Copy,
                                 scale=SCALE).then_inc(a_fold, 1)
            for k in range(2):
                act.wait_ge(v_var, k + 1)
                nc.scalar.activation(nrm[:, 1, :], nrm[:, 0, :], ACT.Sqrt).then_inc(a_std, 1)
                if k == 0:
                    for b in range(B):
                        act.wait_ge(p_xnT, b + 1)
                        nc.scalar.activation(xh[:, b * T:(b + 1) * T], tbank[b][:], ACT.Copy).then_inc(a_xnT, 1)
            act.wait_ge(v_bias, 1)
            for n in range(G * B):
                g, b = n // B, n % B
                act.wait_ge(p_hid, n + 1)
                nc.scalar.activation(gT[:, g, b * T:(b + 1) * T], mbank[n % 4][:], ACT.Gelu,
                                     bias=bias_h[:, g:g + 1]).then_inc(a_hid, 1)

            def high_parts(u, i):
                act.wait_ge(s_q, u + 1)
                for h, own in enumerate((slice(0, DH), slice(DH, P))):
                    last = nc.scalar.activation(QSM[i][h][own, :, :],
                                                bq[own, :].unsqueeze(1).to_broadcast([DH, 2, 512]), ACT.Copy)
                last.then_inc(a_q, 1)

            def high_keys(u, i):
                act.wait_ge(s_k, u + 1)
                nc.scalar.activation(KD[i][0][0:DH, :], bk[0:DH, :], ACT.Copy)
                nc.scalar.activation(KD[i][0][DH:P, :], bk[0:DH, :], ACT.Copy)
                nc.scalar.activation(KD[i][1][0:DH, :], bk[DH:P, :], ACT.Copy)
                nc.scalar.activation(KD[i][1][DH:P, :], bk[DH:P, :], ACT.Copy).then_inc(a_k, 1)

            def values(u, s):
                act.wait_ge(s_v, u + 1)
                nc.scalar.activation(VS[s][:], by[:], ACT.Copy).then_inc(a_v, 1)

            def max_rows(u, i, h):
                act.wait_ge(s_m, 2 * u + h + 1)
                rows = slice(DH, P) if h == 0 else slice(0, DH)
                nc.scalar.activation(QM[i][h][rows, :], (be, bd)[h][rows, :], ACT.Copy).then_inc(a_m, 1)

            def exps(u, i, h):
                for n, (src, c0, w) in enumerate(((st_a, 0, 512), (st_b, 512, 512), (st_c, 1024, 256))):
                    act.wait_ge(s_st, 3 * (2 * u + h) + n + 1)
                    nc.scalar.activation(PR[i][h][:, c0:c0 + w], src[:, 0:w], ACT.Exp).then_inc(a_e, 1)

            def reciprocal(u):
                act.wait_ge(s_l, u + 1)
                if not isinstance(u, int) or u > 0:
                    act.wait_ge(v_r2, u)
                nc.scalar.activation(rden[:], bk[:], ACT.Ln).then_inc(a_r, 1)
                act.wait_ge(a_r, 2 * u + 1)
                nc.scalar.activation(rden[:], rden[:], ACT.Exp, scale=-1.0).then_inc(a_r, 1)

            def step(u, b, first=False, prev=True, more=True, far=True):
                i = b % 2
                if not first:
                    exps(u, i, 0)
                if prev:
                    reciprocal(u - 1)
                if more:
                    values(u + 1, (b + 1) % 4)
                if not first:
                    exps(u, i, 1)
                if far:
                    high_parts(u + 2, i)
                    high_keys(u + 2, i)
                if more:
                    max_rows(u + 1, 1 - i, 0)
                    max_rows(u + 1, 1 - i, 1)

            nc.scalar.preload_act_table_set("natural_log_exp_and_others")
            high_parts(0, 0)
            high_keys(0, 0)
            step(-1, 3, first=True, prev=False)
            for b in range(B):
                step(b, b, prev=b > 0)
            with act.Fori(1, PAIRS - 1) as p:
                for b in range(B):
                    step(B * p + b, b)
            for b in range(B):
                step(B * (PAIRS - 1) + b, b, more=b < B - 1, far=b < B - 2)
            reciprocal(UNITS - 1)

        @block.vector
        def _(dve):
            done = [0]

            def ordered(ins):
                done[0] += 1
                ins.then_inc(v_step, 1)
                dve.wait_ge(v_step, done[0])

            dve.wait_ge(g_const, 4)

            def layer_norm(k, src, dst, signal):
                for t in range(NT):
                    if k == 0 and t % TT == 0:
                        dve.wait_ge(d_x[t // TT], 16)
                    last = nc.vector.bn_stats(stats[:, t, :], src[:, t, :])
                ordered(last)
                for t in range(NT):
                    last = nc.vector.bn_aggr(mv[:, t, :], stats[:, t, :])
                ordered(last)
                var, r, t2 = nrm[:, 0, :], nrm[:, 2, :], nrm[:, 3, :]
                nc.vector.tensor_scalar(var, mv[:, :, 1], LN_EPS, None, ALU.add).then_inc(v_var, 1)
                dve.wait_ge(a_std, k + 1)
                ordered(nc.vector.reciprocal(r, nrm[:, 1, :]))
                ordered(nc.vector.tensor_tensor(t2, r, r, ALU.mult))
                ordered(nc.vector.tensor_tensor(t2, t2, var, ALU.mult))
                ordered(nc.vector.tensor_scalar(t2, t2, -0.5, 1.5, ALU.mult, ALU.add))
                ordered(nc.vector.tensor_tensor(r, r, t2, ALU.mult))
                for t in range(NT):
                    last = nc.vector.tensor_scalar(dst[:, t, :], src[:, t, :], mv[:, t, 0:1], nrm[:, 2, t:t + 1],
                                                   ALU.subtract, ALU.mult)
                    if t == NT - 1:
                        last.then_inc(signal, 1)
                dve.wait_ge(signal, 1)

            dve.wait_ge(p_wdT, 1)
            nc.vector.tensor_copy(wdT, by[:, 0:P]).then_inc(v_wdT, 1)
            layer_norm(0, x_sb, xn, v_xn)
            for n in range(4):
                dve.wait_ge(a_fold, n + 1)
                o = (2, 4)[n // 2]
                rs = slice(4 * (n % 2), 4 * (n % 2) + 4)
                nc.vector.tensor_tensor(w_all[:, rs, o + 1, :], mbank[n][:].rearrange("p (r c) -> p r c", c=P),
                                        w_all[:, rs, o, :].bitcast(F32), ALU.subtract).then_inc(v_fold, 1)
            dve.wait_ge(a_fold, 5)
            nc.vector.scalar_tensor_tensor(out=w_all[:, :, 1, :], in0=wq_raw.rearrange("p (r c) -> p r c", c=P),
                                           scalar=SCALE, in1=w_all[:, :, 0, :].bitcast(F32), op0=ALU.mult,
                                           op1=ALU.subtract).then_inc(v_fold, 1)
            for b in range(B):
                c = slice(b * T, (b + 1) * T)
                dve.wait_ge(a_xnT, b + 1)
                nc.vector.tensor_tensor(xl[:, c], tbank[b][:], xh[:, c].bitcast(F32), ALU.subtract)
                nc.vector.tensor_copy(xnT[:, c], tbank[b][:]).then_inc(v_xnT, 1)
            layer_norm(1, xn, xhat, v_xhat)
            dve.wait_ge(p_rows, 1)
            nc.vector.tensor_copy(cols8[:].rearrange("p a e -> p (a e)"), mbank[0][:, 0:3 * E]).then_inc(v_cols, 1)
            dve.wait_ge(v_cols, 1)
            dve.wait_ge(d_small, 16 * 5)
            nc.vector.tensor_tensor(w1s, w1_sb, cols8[:, 1, :].unsqueeze(2).to_broadcast([P, E, HID]), ALU.mult)
            nc.vector.tensor_tensor(w1b, w1_sb, cols8[:, 2, :].unsqueeze(2).to_broadcast([P, E, HID]),
                                    ALU.mult).then_inc(v_cols, 1)
            for b in range(B):
                dve.wait_ge(p_xhatT, b + 1)
                nc.vector.tensor_copy(xhatT[:, b * T:(b + 1) * T], tbank[b][:]).then_inc(v_xhatT, 1)
            dve.wait_ge(p_bias, 1)
            nc.vector.tensor_copy(bias_h[:], mbank[1][:, 0:G]).then_inc(v_bias, 1)
            dve.wait_ge(p_logit, 1)
            ordered(nc.vector.tensor_copy(logit[:].rearrange("p t e -> p (t e)"), mbank[2][:, 0:NT * E]))
            ordered(nc.vector.tensor_reduce(best[:, 0, :], logit[:], mybir.AxisListType.X, ALU.max))
            ordered(nc.vector.tensor_tensor(pick[:], logit[:], best[:, 0, :].unsqueeze(2).to_broadcast([P, NT, E]),
                                            ALU.is_ge))
            ordered(nc.vector.tensor_tensor(pick[:], pick[:], order[:].unsqueeze(1).to_broadcast([P, NT, E]),
                                            ALU.mult))
            ordered(nc.vector.tensor_reduce(best[:, 1, :], pick[:], mybir.AxisListType.X, ALU.max))
            nc.vector.tensor_tensor(pick[:], pick[:], best[:, 1, :].unsqueeze(2).to_broadcast([P, NT, E]),
                                    ALU.is_ge).then_inc(v_mask, 1)
            for b in range(B):
                dve.wait_ge(p_maskT, b + 1)
                nc.vector.tensor_copy(mask_new[:, b * T:(b + 1) * T], tbank[b][0:E, :]).then_inc(v_maskT, 1)
            for n in range(G * B):
                g, b = n // B, n % B
                dve.wait_ge(p_exp, n + 1)
                dve.wait_ge(a_hid, n + 1)
                c = gT[:, g, b * T:(b + 1) * T]
                nc.vector.tensor_tensor(c, tbank[n % 4][:], c, ALU.mult).then_inc(v_gm, 1)

            def low_parts(u, i):
                dve.wait_ge(a_q, u + 1)
                for h in range(2):
                    own = slice(0, DH) if h == 0 else slice(DH, P)
                    other = slice(DH, P) if h == 0 else slice(0, DH)
                    last = nc.vector.tensor_tensor(QS[i][h][other, :], bq[own, :], QS[i][h][own, :].bitcast(F32),
                                            ALU.subtract)
                last.then_inc(v_q, 1)

            def low_keys(u, i):
                dve.wait_ge(a_k, u + 1)
                for h in range(2):
                    own = slice(0, DH) if h == 0 else slice(DH, P)
                    last = nc.vector.tensor_tensor(KL[i][h][own, :], bk[own, :], KD[i][h][own, :].bitcast(F32),
                                                   ALU.subtract)
                last.then_inc(v_k, 1)

            def maxima(u, h):
                base = 3 * (2 * u + h)
                for n, parts in enumerate((((bd, 0, 3),), ((be, 0, 2), (be, 384, 0)), ((bd, 0, 1),))):
                    dve.wait_ge(s_x, base + n + 1)
                    dve.sem_inc(v_turn, 1)
                    for src, c0, j in parts:
                        w = P * (j + 1)
                        last = nc.vector.tensor_tensor_reduce(
                            out=src[:, c0:c0 + w], in0=src[:, c0:c0 + w], in1=neg_qk[:, 512 - w:512], scale=1.0,
                            scalar=-3.0e38, op0=ALU.add, op1=ALU.max, accum_out=mx[h][:, j:j + 1])
                    last.then_inc(v_x, 1)

            dve.wait_ge(d_mask, 16)

            def invert(u):
                dve.wait_ge(a_r, 2 * u + 2)
                if not isinstance(u, int) or u > 0:
                    dve.wait_ge(v_n, u)
                nc.vector.tensor_tensor(scratch[:], bk[:], rden[:], ALU.mult).then_inc(v_r, 1)
                dve.wait_ge(v_r, u + 1)
                nc.vector.scalar_tensor_tensor(out=scratch[:], in0=scratch[:], scalar=2.0, in1=rden[:],
                                               op0=ALU.subtract, op1=ALU.mult).then_inc(v_r2, 1)

            def normalise(u, p, b):
                dve.wait_ge(v_r2, u + 1)
                dve.wait_ge(s_y, u + 1)
                nc.vector.scalar_tensor_tensor(out=yT[:, p, b * T:(b + 1) * T], in0=by[:], scalar=-1.0,
                                               in1=scratch[:], op0=ALU.mult, op1=ALU.mult).then_inc(v_n, 1)

            def step(u, p, b, first=False, norm=True, more=True, far=True):
                i = b % 2
                if norm:
                    invert(u - 1)
                if more:
                    maxima(u + 1, 0)
                    maxima(u + 1, 1)
                if far:
                    low_parts(u + 2, i)
                    low_keys(u + 2, i)
                if norm:
                    normalise(u - 1, p if b else p - 1, (b - 1) % B)

            low_parts(0, 0)
            low_keys(0, 0)
            step(-1, 0, 3, norm=False)
            for b in range(B):
                step(b, 0, b, norm=b > 0)
            with dve.Fori(1, PAIRS - 1) as p:
                for b in range(B):
                    step(B * p + b, p, b)
            for b in range(B):
                step(B * (PAIRS - 1) + b, PAIRS - 1, b, more=b < B - 1, far=b < B - 2)
            invert(UNITS - 1)
            normalise(UNITS - 1, PAIRS - 1, B - 1)
            for b in range(B):
                dve.wait_ge(s_o, b + 1)
                if b >= 2:
                    dve.wait_ge(d_out[b % 2], 16)
                dve.wait_ge(d_xa[b], 16)
                nc.vector.tensor_tensor(res[b % 2][:], tbank[b][:], x_again[b], ALU.add).then_inc(v_o, 1)

        @block.tensor
        def _(pe):
            mm = nc.tensor.matmul
            pe.wait_ge(g_const, 4)
            pe.wait_ge(d_wd, 16)
            nc.tensor.transpose(by[:, 0:P], wd, ident[:]).then_inc(p_wdT, 1)
            pe.wait_ge(v_wdT, 1)
            pe.wait_ge(d_kv, 16)
            for n in range(4):
                mm(mbank[n][:], wdT, kv_up[:, n * 512:(n + 1) * 512], start=True, stop=True).then_inc(p_fold, 1)
            pe.wait_ge(v_xn, 1)
            for b in range(B):
                for j in range(TT):
                    last = nc.tensor.transpose(tbank[b][:, j * P:(j + 1) * P], xn[:, b * TT + j, :], ident[:])
                last.then_inc(p_xnT, 1)
            pe.wait_ge(v_fold, 4)
            pe.wait_ge(d_small, 16 * 5)
            for a in range(3):
                last = nc.tensor.transpose(mbank[0][:, a * E:(a + 1) * E], rows8[:, a, :], ident[0:E, 0:E])
            last.then_inc(p_rows, 1)
            pe.wait_ge(v_cols, 1)
            pe.wait_ge(v_xnT, B)
            for t in range(NT):
                last = mm(mbank[2][:, t * E:(t + 1) * E], xnT[:, t * P:(t + 1) * P], cols8[:, 0, :], start=True, stop=True)
            last.then_inc(p_logit, 1)
            pe.wait_ge(v_xhat, 1)
            for b in range(B):
                for j in range(TT):
                    last = nc.tensor.transpose(tbank[b][:, j * P:(j + 1) * P], xhat[:, b * TT + j, :], ident[:])
                last.then_inc(p_xhatT, 1)
            pe.wait_ge(v_cols, 2)
            for g in range(G):
                mm(mbank[1][:, g:g + 1], w1b.rearrange("p e h -> p (e h)")[:, g * P:(g + 1) * P],
                   ones[:, 0:1], start=True, stop=False)
                last = mm(mbank[1][:, g:g + 1], b1_rows[:], ident[0:G, g:g + 1], start=False, stop=True)
            last.then_inc(p_bias, 1)
            pe.wait_ge(v_bias, 1)
            pe.wait_ge(v_mask, 1)
            for n in range(G * B):
                g, b = n // B, n % B
                if g == 0:
                    pe.wait_ge(v_xhatT, b + 1)
                if n >= 4:
                    pe.wait_ge(a_hid, n - 3)
                mm(mbank[n % 4][:], w1s.rearrange("p e h -> p (e h)")[:, g * P:(g + 1) * P],
                   xhatT[:, b * T:(b + 1) * T], start=True, stop=True).then_inc(p_hid, 1)
            for b in range(B):
                for j in range(TT):
                    last = nc.tensor.transpose(tbank[b][0:E, j * P:(j + 1) * P], pick[:, b * TT + j, :], ident[:])
                last.then_inc(p_maskT, 1)
            for n in range(G * B):
                g, b = n // B, n % B
                if n < B:
                    pe.wait_ge(v_maskT, B)
                else:
                    pe.wait_ge(v_gm, n - 3)
                mm(tbank[n % 4][:], expand[:, g * P:(g + 1) * P], mask_new[:, b * T:(b + 1) * T],
                   start=True, stop=True).then_inc(p_exp, 1)
            pe.wait_ge(v_gm, G * B)
            pe.wait_ge(a_hid, G * B)

            def project_q(p, b):
                c = slice(b * T, (b + 1) * T)
                for n, (w, xx) in enumerate(((0, xh), (0, xl), (1, xh))):
                    last = mm(bq[:], w_qk[:, w, :], xx[:, c], start=n == 0, stop=n == 2)
                last.then_inc(s_q, 1)

            def project_k(p, b):
                c = slice(b * T, (b + 1) * T)
                for n, (w, xx) in enumerate(((2, xh), (2, xl), (3, xh))):
                    last = mm(bk[:], w_qk[:, w, :], xx[:, c], start=n == 0, stop=n == 2)
                last.then_inc(s_k, 1)

            def project_v(b):
                for j in range(TT):
                    c = slice(b * T + j * P, b * T + (j + 1) * P)
                    for n, (xx, w) in enumerate(((xh, 0), (xh, 1), (xl, 0))):
                        last = mm(by[:, j * P:(j + 1) * P], xx[:, c], w_v[:, w, :], start=n == 0, stop=n == 2)
                last.then_inc(s_v, 1)

            def score_piece(i, h, dst, parts):
                for c0, j in parts:
                    w = T - P * j
                    k = slice(j * P, (j + 1) * P)
                    mm(dst[:, c0:c0 + w], KD[i][h][:, k], QS[i][h][:, T - w:T], start=True, stop=False)
                    last = mm(dst[:, c0:c0 + w], KL[i][h][:, k], QM[i][h][:, T - w:T], start=False, stop=True)
                last.then_inc(s_st, 1)

            def all_scores(u, i, h):
                pe.wait_ge(a_m, 2 * u + h + 1)
                for n, (dst, parts) in enumerate(((st_a, ((0, 0),)), (st_b, ((0, 1), (384, 3))), (st_c, ((0, 2),)))):
                    s = 3 * (2 * u + h) + n - 2
                    if not isinstance(s, int) or s > 0:
                        pe.wait_ge(a_e, s)
                    score_piece(i, h, dst, parts)

            def max_piece(i, h, dst, parts):
                for c0, j in parts:
                    w = P * (j + 1)
                    last = mm(dst[:, c0:c0 + w], QS[i][h][:, j * P:(j + 1) * P], KD[i][h][:, 0:w], start=True, stop=True)
                last.then_inc(s_x, 1)

            def pv(b, j):
                i, s = b % 2, b % 4
                w = T - P * j
                c0 = (0, 512, 1024, 896)[j]
                for h in range(2):
                    last = mm(by[h * DH:(h + 1) * DH, P * j:T], VS[s][:, j * P + h * DH:j * P + (h + 1) * DH],
                              PR[i][h][:, c0:c0 + w], start=j == 0, stop=j == TT - 1)
                if j == TT - 1:
                    last.then_inc(s_y, 1)

            def denominators(b):
                i = b % 2
                for h in range(2):
                    mm(bk[h * DH:(h + 1) * DH, 0:P], ones[:], PR[i][h][:, 0:P], start=True, stop=True)
                    last = mm(bk[h * DH:(h + 1) * DH, P:T], ones[:], PS[i][h][:], start=True, stop=True)
                last.then_inc(s_l, 1)

            def spread_max(h):
                mm((be, bd)[h][:], ones_r[:], DG[h][:].rearrange("p t c -> p (t c)"), start=True, stop=True).then_inc(s_m, 1)

            def step(u, p, b, first=False, prev=True, more=True, far=True):
                i = b % 2
                nb, fb, pb = (b + 1) % B, (b + 2) % B, (b - 1) % B
                np_ = p if b < B - 1 else p + 1
                fp = p if b < B - 2 else p + 1
                if not first:
                    all_scores(u, i, 0)
                if prev:
                    if far or more:
                        pe.wait_ge(v_k, u + 2)
                    else:
                        pe.wait_ge(v_r, u - 1)
                    pe.wait_ge(g_s, 2 * u)
                    denominators(pb)
                if more:
                    pe.wait_ge(d_wv, 16 * (np_ + 1))
                    if prev and not (isinstance(u, int) and u < 2):
                        pe.wait_ge(v_n, u - 1)
                    project_v(nb)
                if not first:
                    all_scores(u, i, 1)
                if more:
                    pe.wait_ge(v_q, u + 2)
                    pe.wait_ge(v_k, u + 2)
                    if not first:
                        pe.wait_ge(a_m, 2 * u + 2)
                    max_piece(1 - i, 0, bd, ((0, 3),))
                    max_piece(1 - i, 0, be, ((0, 2), (384, 0)))
                if far:
                    pe.wait_ge(d_wqk, 16 * (fp + 1))
                    pe.wait_ge(v_q, u + 2)
                    project_q(fp, fb)
                if more:
                    pe.wait_ge(v_x, 6 * (u + 1) + 1)
                    max_piece(1 - i, 0, bd, ((0, 1),))
                if far:
                    if prev:
                        pe.wait_ge(v_r, u)
                    project_k(fp, fb)
                if more:
                    pe.wait_ge(v_x, 6 * (u + 1) + 3)
                    max_piece(1 - i, 1, bd, ((0, 3),))
                    max_piece(1 - i, 1, be, ((0, 2), (384, 0)))
                if prev:
                    if more:
                        pe.wait_ge(a_v, u + 2)
                    else:
                        pe.wait_ge(v_n, u - 1)
                    pe.wait_ge(g_s, 2 * u)
                    pv(pb, 0)
                if more:
                    pe.wait_ge(v_x, 6 * (u + 1) + 4)
                    max_piece(1 - i, 1, bd, ((0, 1),))
                if prev:
                    pv(pb, 1)
                if more:
                    pe.wait_ge(g_d, 2 * (u + 1) + 1)
                    pe.wait_ge(v_x, 6 * (u + 1) + 5)
                    spread_max(0)
                if prev:
                    pv(pb, 2)
                    pv(pb, 3)
                if more:
                    pe.wait_ge(g_d, 2 * (u + 1) + 2)
                    pe.wait_ge(v_x, 6 * (u + 1) + 6)
                    spread_max(1)

            pe.wait_ge(d_wqk, 16)
            project_q(0, 0)
            project_k(0, 0)
            step(-1, -1, B - 1, first=True, prev=False)
            for b in range(B):
                step(b, 0, b, prev=b > 0)
            with pe.Fori(1, PAIRS - 1) as p:
                for b in range(B):
                    step(B * p + b, p, b)
            for b in range(B):
                step(B * (PAIRS - 1) + b, PAIRS - 1, b, more=b < B - 1, far=b < B - 2)
            pe.wait_ge(g_s, 2 * UNITS)
            pe.wait_ge(v_n, UNITS - 1)
            for j in range(TT):
                pv(B - 1, j)
            pe.wait_ge(g_s, 2 * UNITS)
            pe.wait_ge(v_r, UNITS - 1)
            denominators(B - 1)

            pe.wait_ge(d_late, 16 * 4)
            pe.wait_ge(v_n, UNITS)
            for b in range(B):
                for j in range(TT):
                    c = slice(b * T + j * P, b * T + (j + 1) * P)
                    dst = tbank[b][:, j * P:(j + 1) * P]
                    mm(dst, maskT[:, c], b2_sb[:], start=True, stop=False)
                    for g in range(G):
                        mm(dst, gT[:, g, c], w2_sb[:, g, :], start=False, stop=False)
                    for r in range(PAIRS):
                        last = mm(dst, yT[:, r, c], wout_sb[:, r, :], start=False, stop=r == PAIRS - 1)
                last.then_inc(s_o, 1)


_INS = ["L0_attn_x", "L0_attn_w_kv_down", "L0_attn_w_kv_up", "L0_attn_w_q", "L0_attn_w_out", "L0_ffn_Wg",
        "L0_ffn_ln_scale", "L0_ffn_ln_bias", "L0_ffn_W1", "L0_ffn_b1", "L0_ffn_W2", "L0_ffn_b2"]


def kernel(**inputs):
    import numpy as _np
    import concourse.bacc as _bacc
    from concourse import mybir as _mybir
    from concourse.bass_utils import run_bass_kernel_spmd as _run

    nc = _bacc.Bacc("TRN2", target_bir_lowering=False, num_devices=1)
    arrays, args = {}, []
    for name in _INS:
        a = _np.ascontiguousarray(inputs[name])
        arrays[f"in_{name}_dram"] = a
        args.append(nc.dram_tensor(f"in_{name}_dram", a.shape, _mybir.dt.from_np(a.dtype), kind="ExternalInput").ap())
    shape = inputs["L0_attn_x"].shape
    dt = _mybir.dt.from_np(_np.dtype("float32"))
    args.append(nc.dram_tensor("out_0_dram", shape, dt, kind="ExternalOutput").ap())
    attention_and_experts(nc, *args)
    r = _run(nc, [arrays], core_ids=[0])
    return r.results[0]["out_0_dram"]
```

```python
import concourse.bass as bass
from concourse import mybir
from contextlib import ExitStack

F32 = mybir.dt.float32
F32R = mybir.dt.float32r
BF16 = mybir.dt.bfloat16
ALU = mybir.AluOpType
ACT = mybir.ActivationFunctionType

P = 128
NEG = -1.0e30
LN_EPS = 1e-5


def attention_and_experts(nc, x, w_kv_down, w_kv_up, w_q, w_out, wg, ln_scale, ln_bias, w1, b1, w2, b2, out):
    B, T, C = x.shape
    HD = w_q.shape[1]
    E, _, HID = w1.shape
    DH = 64
    PAIRS = HD // P
    TT = T // P
    NT = B * TT
    TOK = B * T
    G = E * HID // P
    EG = E // G
    UNITS = PAIRS * B
    SCALE = float(DH) ** -0.5
    assert C == P and T == 512 and w_kv_down.shape[1] == P and B == 4

    with ExitStack() as ctx:
        def sb(name, shape, dt=F32):
            return ctx.enter_context(nc.sbuf_tensor(name, shape, dt))

        def bank(name):
            return ctx.enter_context(nc.psum_tensor(name, [P, 512], F32))

        def sem(name):
            return ctx.enter_context(nc.semaphore(name))

        yT = sb("yT", [P, PAIRS, TOK])
        xn = yT[:, 7, :].rearrange("p (t c) -> p t c", c=C)
        xnT = yT[:, 5, :]
        kv_up = yT[:, 3, :]
        wq_raw = yT[:, 2, 0:HD]
        w1_sb, w1b = (yT[:, 2, HD + n * E * HID:HD + (n + 1) * E * HID].rearrange("p (e h) -> p e h", e=E)
                      for n in range(2))
        x_sb = yT[:, 1, :].rearrange("p (t c) -> p t c", c=C)
        wd, wdT = yT[:, 2, TOK - 2 * P:TOK - P], yT[:, 2, TOK - P:TOK]
        xh = sb("xh", [P, TOK], F32R)
        xl = sb("xl", [P, TOK], F32R)
        w_all = sb("w_all", [P, PAIRS, 6, P], F32R)
        w_qk = sb("w_qk", [P, 4, P], F32R)
        w_v = sb("w_v", [P, 2, P], F32R)
        xhat = sb("xhat", [P, NT, C])
        w1s = sb("w1s", [P, E, HID])
        w2_sb = sb("w2_sb", [P, G, C])
        b2_sb = sb("b2_sb", [E, C])
        rows8 = sb("rows8", [E, 3, C])
        cols8 = sb("cols8", [P, 3, E])
        b1_rows = sb("b1_rows", [G, P])
        bias_h = sb("bias_h", [P, G])
        ident = sb("ident", [P, P])
        neg_qk = sb("neg_qk", [P, 512])
        ones = sb("ones", [P, DH])
        ones_r = sb("ones_r", [P, P], F32R)
        expand = sb("expand", [E, E * HID], F32R)
        order = sb("order", [P, E])
        stats = sb("stats", [P, NT, 6])
        mv = sb("mv", [P, NT, 2])
        nrm = sb("nrm", [P, 4, NT])
        logit = sb("logit", [P, NT, E])
        pick = sb("pick", [P, NT, E])
        best = sb("best", [P, 2, NT])
        QSM = [[sb(f"QSM{i}{h}", [P, 2, 512], F32R) for h in range(2)] for i in range(2)]
        QS = [[q[:, 0, :] for q in row] for row in QSM]
        QM = [[q[:, 1, :] for q in row] for row in QSM]
        KD = [[sb(f"KD{i}{h}", [P, 512], F32R) for h in range(2)] for i in range(2)]
        KL = [[sb(f"KL{i}{h}", [P, 512], F32R) for h in range(2)] for i in range(2)]
        PR = [[sb(f"PR{i}{h}", [P, 1280]) for h in range(2)] for i in range(2)]
        PS = [[sb(f"PS{i}{h}", [P, 384]) for h in range(2)] for i in range(2)]
        VS = [sb(f"VS{i}", [P, 512]) for i in range(4)]
        DG = [sb(f"DG{h}", [P, TT, P], F32R) for h in range(2)]
        mx = [sb(f"mx{h}", [P, TT]) for h in range(2)]
        scratch = sb("scratch", [P, 512])
        rden = sb("rden", [P, 512])
        wout_sb = PR[0][1][:, 0:PAIRS * C].rearrange("p (r c) -> p r c", c=C)
        x_again = [PR[0][0][:, 0:512], PR[0][0][:, 512:1024], VS[2][:], VS[0][:]]
        res = [VS[1], scratch]
        maskT = xl[0:E, :]
        folded = w_all[:].bitcast(F32).rearrange("p r w c -> p (r w c)")
        gT = folded[:, 0:G * TOK].rearrange("p (g t) -> p g t", g=G)
        xhatT = folded[:, G * TOK:(G + 1) * TOK]

        st_a, st_b, st_c = bank("st_a"), bank("st_b"), bank("st_c")
        bd, be = bank("bd"), bank("be")
        bq, bk = bank("bq"), bank("bk")
        by = bank("by")

        d_x = [sem(f"d_x{b}") for b in range(B)]
        d_wd = sem("d_wd")
        d_kv = sem("d_kv")
        d_wq = sem("d_wq")
        d_small = sem("d_small")
        d_late = sem("d_late")
        d_xa = [sem(f"d_xa{b}") for b in range(B)]
        d_wqk = sem("d_wqk")
        d_wv = sem("d_wv")
        d_out = [sem(f"d_out{i}") for i in range(2)]
        g_const = sem("g_const")
        g_step = sem("g_step")
        v_step = sem("v_step")
        p_wdT, a_wdT = sem("p_wdT"), sem("a_wdT")
        p_fold, a_fold, v_fold = sem("p_fold"), sem("a_fold"), sem("v_fold")
        v_var, a_log, a_std = sem("v_var"), sem("a_log"), sem("a_std")
        v_xn, p_xnT, a_xnT, v_xl = sem("v_xn"), sem("p_xnT"), sem("a_xnT"), sem("v_xl")
        v_xhat = sem("v_xhat")
        p_rows, v_cols, g_w1 = sem("p_rows"), sem("v_cols"), sem("g_w1")
        p_logit, v_logit, v_pick = sem("p_logit"), sem("v_logit"), sem("v_pick")
        s_q, s_k, s_v = sem("s_q"), sem("s_k"), sem("s_v")
        a_q, a_k, a_v = sem("a_q"), sem("a_k"), sem("a_v")
        v_q, v_k = sem("v_q"), sem("v_k")
        s_x, v_x = sem("s_x"), sem("v_x")
        v_turn = sem("v_turn")
        g_d, s_m, a_m = sem("g_d"), sem("s_m"), sem("a_m")
        s_st, a_e = sem("s_st"), sem("a_e")
        g_turn = sem("g_turn")
        g_s1 = sem("g_s1")
        g_s = sem("g_s")
        s_y, s_l = sem("s_y"), sem("s_l")
        a_r, v_r, v_r2 = sem("a_r"), sem("v_r"), sem("v_r2")
        v_n = sem("v_n")
        p_xhatT, v_xhatT = sem("p_xhatT"), sem("v_xhatT")
        p_maskT, v_maskT = sem("p_maskT"), sem("v_maskT")
        p_hid, a_hid = sem("p_hid"), sem("a_hid")
        p_exp, v_gm = sem("p_exp"), sem("v_gm")
        s_o, v_o = sem("s_o"), sem("v_o")

        x_v = x.rearrange("b (j p) c -> p (b j) c", p=P)
        out_v = out.rearrange("b (j p) c -> p (b j) c", p=P)

        block = ctx.enter_context(nc.Block())

        tbank = [by, st_a, st_b, st_c]
        mbank = [bd, bq, be, bk]
        FOLDS = ((2, 0), (4, 0), (2, 4), (4, 4))
        hbank = [bd, be, bq]
        ebank = [st_a, st_b]
        obank = [st_c, bk]

        @block.sync
        def _(sp):
            for b in range(B):
                sp.dma_start(x_sb[:, b * TT:(b + 1) * TT, :], x_v[:, b * TT:(b + 1) * TT, :]).then_inc(d_x[b], 16)
            sp.dma_start(wq_raw, w_q).then_inc(d_wq, 16)
            sp.dma_start(rows8[:, 0, :], wg).then_inc(d_small, 16)
            sp.dma_start(rows8[:, 1, :], ln_scale).then_inc(d_small, 16)
            sp.dma_start(rows8[:, 2, :], ln_bias).then_inc(d_small, 16)
            sp.dma_start(b1_rows[:], b1.rearrange("(g e) h -> g (e h)", g=G)).then_inc(d_small, 16)
            sp.dma_start(w1_sb, w1.rearrange("e d h -> d e h")).then_inc(d_small, 16)
            sp.dma_start(w2_sb[:], w2.rearrange("(g e) h c -> (e h) g c", g=G)).then_inc(d_late, 16)
            sp.dma_start(b2_sb[:], b2).then_inc(d_late, 16)
            sp.wait_ge(v_fold, 3)
            sp.dma_start(w_qk[:].bitcast(F32), w_all[:, 0, 0:4, :].bitcast(F32)).then_inc(d_wqk, 16)
            sp.dma_start(w_v[:].bitcast(F32), w_all[:, 0, 4:6, :].bitcast(F32)).then_inc(d_wv, 16)
            sp.wait_ge(v_fold, 5)
            with sp.Fori(1, PAIRS) as p:
                sp.wait_ge(s_k, B * p)
                sp.dma_start(w_qk[:].bitcast(F32), w_all[:, p, 0:4, :].bitcast(F32)).then_inc(d_wqk, 16)
                sp.wait_ge(s_v, B * p)
                sp.dma_start(w_v[:].bitcast(F32), w_all[:, p, 4:6, :].bitcast(F32)).then_inc(d_wv, 16)
            sp.wait_ge(s_l, UNITS - 1)
            sp.wait_ge(s_y, UNITS - 1)
            sp.dma_start(wout_sb, w_out.rearrange("(r p) c -> p r c", p=P)).then_inc(d_late, 16)
            for b in range(B):
                sp.dma_start(x_again[b].rearrange("p (t c) -> p t c", c=C), x_v[:, b * TT:(b + 1) * TT, :]).then_inc(d_xa[b], 16)
            for b in range(B):
                sp.wait_ge(v_o, b + 1)
                sp.dma_start(out_v[:, b * TT:(b + 1) * TT, :],
                             res[b % 2][:].rearrange("p (t c) -> p t c", c=C)).then_inc(d_out[b % 2], 16)
            for i in range(2):
                sp.wait_ge(d_out[i], 16 * B // 2)

        @block.gpsimd
        def _(pool):
            done = [0]

            def ordered(ins):
                done[0] += 1
                ins.then_inc(g_step, 1)
                pool.wait_ge(g_step, done[0])

            ordered(nc.gpsimd.memset(ident[:], 0.0))
            nc.gpsimd.affine_select(out=ident[:], in_=ident[:], compare_op=ALU.not_equal, fill=1.0, base=0,
                                    pattern=[[-1, P]], channel_multiplier=1).then_inc(g_const, 1)
            ordered(nc.gpsimd.memset(neg_qk[:], 0.0))
            nc.gpsimd.affine_select(out=neg_qk[:, 384:512], in_=neg_qk[:, 384:512], compare_op=ALU.is_ge,
                                    fill=NEG, base=0, pattern=[[-1, P]], channel_multiplier=1).then_inc(g_const, 1)
            wide = scratch[0:E, 0:E * HID]
            ordered(nc.gpsimd.memset(wide, 0.0))
            ordered(nc.gpsimd.affine_select(out=wide.rearrange("e (f h) -> e f h", f=E),
                                            in_=wide.rearrange("e (f h) -> e f h", f=E),
                                            compare_op=ALU.not_equal, fill=1.0, base=0,
                                            pattern=[[-1, E], [0, HID]], channel_multiplier=1))
            nc.gpsimd.tensor_copy(expand[:], wide).then_inc(g_const, 1)
            nc.gpsimd.memset(ones[:], 1.0)
            nc.gpsimd.memset(ones_r[:].bitcast(F32), 1.0)
            for e in range(E):
                last = nc.gpsimd.memset(order[:, e:e + 1], float(E - e))
            ordered(last)
            for i in range(2):
                ordered(nc.gpsimd.memset(KL[i][0][DH:P, :].bitcast(F32), -1.0 / DH))
                last = nc.gpsimd.memset(KL[i][1][0:DH, :].bitcast(F32), -1.0 / DH)
                if i == 0:
                    ordered(last)
            last.then_inc(g_const, 1)
            pool.wait_ge(g_const, 4)
            pool.wait_ge(d_small, 16 * 5)
            pool.wait_ge(v_cols, 1)
            for dst, a in ((w1s[:], 1), (w1b, 2)):
                nc.gpsimd.tensor_tensor(dst, w1_sb, cols8[:, a, :].unsqueeze(2).to_broadcast([P, E, HID]),
                                        ALU.mult).then_inc(g_w1, 1)

            nsum = [0]

            def diagonal(u, h):
                pool.wait_ge(v_x, 3 * (2 * u + h + 1))
                nc.gpsimd.tensor_tensor(DG[h][:], ident[:].unsqueeze(1).to_broadcast([P, TT, P]),
                                        mx[h][:].unsqueeze(2).to_broadcast([P, TT, P]),
                                        ALU.mult).then_inc(g_d, 1)

            def sums(u, i, h):
                pr, ps = PR[i][h], PS[i][h]
                pool.wait_ge(a_e, 3 * (2 * u + h + 1))
                pool.sem_inc(g_turn, 1)
                base = 4 * (2 * u + h)
                for blocks in (pr[:, 0:1024].rearrange("p (k c) -> p k c", k=2)[:, :, 0:P],
                               pr[:, 896:1152].rearrange("p (k c) -> p k c", k=2)):
                    nc.gpsimd.affine_select(out=blocks, in_=blocks, compare_op=ALU.is_ge, fill=0.0, base=0,
                                            pattern=[[0, 2], [1, P]], channel_multiplier=-1).then_inc(g_s1, 1)
                pool.wait_ge(g_s1, base + 2)
                nc.gpsimd.tensor_tensor(ps[:, 0:384], pr[:, 128:512], pr[:, 512:896], ALU.add).then_inc(g_s1, 1)
                pool.wait_ge(g_s1, base + 3)
                nc.gpsimd.tensor_tensor(ps[:, 128:384], ps[:, 128:384], pr[:, 1024:1280], ALU.add).then_inc(g_s1, 1)
                pool.wait_ge(g_s1, base + 4)
                nc.gpsimd.tensor_tensor(ps[:, 256:384], ps[:, 256:384], pr[:, 896:1024], ALU.add).then_inc(g_s, 1)

            def step(u, i, first=False, more=True):
                if not first:
                    sums(u, i, 0)
                    sums(u, i, 1)
                if more:
                    diagonal(u + 1, 0)
                    diagonal(u + 1, 1)

            step(-1, 1, first=True)
            for b in range(B):
                step(b, b % 2)
            with pool.Fori(1, PAIRS - 1) as p:
                for b in range(B):
                    step(B * p + b, b % 2)
            for b in range(B):
                step(B * (PAIRS - 1) + b, b % 2, more=b < B - 1)

        @block.scalar
        def _(act):
            nc.scalar.preload_act_table_set("natural_log_exp_and_others")
            act.dma_start(wd, w_kv_down).then_inc(d_wd, 16)
            act.dma_start(kv_up, w_kv_up).then_inc(d_kv, 16)
            act.wait_ge(p_wdT, 1)
            nc.scalar.activation(wdT, by[:, 0:P], ACT.Copy).then_inc(a_wdT, 1)

            def rsqrt(k):
                act.wait_ge(v_var, k + 1)
                nc.scalar.activation(nrm[:, 1, :], nrm[:, 0, :], ACT.Ln).then_inc(a_log, 1)
                act.wait_ge(a_log, k + 1)
                nc.scalar.activation(nrm[:, 2, :], nrm[:, 1, :], ACT.Exp, scale=-0.5).then_inc(a_std, 1)

            def high_folded(n):
                act.wait_ge(p_fold, n + 1)
                o, r = FOLDS[n]
                nc.scalar.activation(w_all[:, r:r + 4, o, :], mbank[n][:].rearrange("p (r c) -> p r c", c=P),
                                     ACT.Copy).then_inc(a_fold, 1)

            rsqrt(0)
            act.wait_ge(d_wq, 16)
            nc.scalar.activation(w_all[:, :, 0, :], wq_raw.rearrange("p (r c) -> p r c", c=P), ACT.Copy,
                                 scale=SCALE).then_inc(a_fold, 1)
            for n in range(4):
                high_folded(n)
            for b in range(B):
                act.wait_ge(p_xnT, b + 1)
                nc.scalar.activation(xh[:, b * T:(b + 1) * T], tbank[b][:], ACT.Copy)
                nc.scalar.activation(xnT[:, b * T:(b + 1) * T], tbank[b][:], ACT.Copy).then_inc(a_xnT, 1)

            def high_parts(u, i):
                act.wait_ge(s_q, u + 1)
                for h, own in enumerate((slice(0, DH), slice(DH, P))):
                    last = nc.scalar.activation(QSM[i][h][own, :, :],
                                                bq[own, :].unsqueeze(1).to_broadcast([DH, 2, 512]), ACT.Copy)
                last.then_inc(a_q, 1)

            def high_keys(u, i):
                act.wait_ge(s_k, u + 1)
                nc.scalar.activation(KD[i][0][0:DH, :], bk[0:DH, :], ACT.Copy)
                nc.scalar.activation(KD[i][0][DH:P, :], bk[0:DH, :], ACT.Copy)
                nc.scalar.activation(KD[i][1][0:DH, :], bk[DH:P, :], ACT.Copy)
                nc.scalar.activation(KD[i][1][DH:P, :], bk[DH:P, :], ACT.Copy).then_inc(a_k, 1)

            def values(u, s):
                act.wait_ge(s_v, u + 1)
                nc.scalar.activation(VS[s][:], by[:], ACT.Copy).then_inc(a_v, 1)

            def max_rows(u, i, h):
                act.wait_ge(s_m, 2 * u + h + 1)
                rows = slice(DH, P) if h == 0 else slice(0, DH)
                nc.scalar.activation(QM[i][h][rows, :], (be, bd)[h][rows, :], ACT.Copy).then_inc(a_m, 1)

            def exps(u, i, h):
                for n, (src, c0, w) in enumerate(((st_a, 0, 512), (st_b, 512, 512), (st_c, 1024, 256))):
                    act.wait_ge(s_st, 3 * (2 * u + h) + n + 1)
                    nc.scalar.activation(PR[i][h][:, c0:c0 + w], src[:, 0:w], ACT.Exp).then_inc(a_e, 1)

            def reciprocal(u):
                act.wait_ge(s_l, u + 1)
                if not isinstance(u, int) or u > 0:
                    act.wait_ge(v_r2, u)
                nc.scalar.activation(rden[:], bk[:], ACT.Ln).then_inc(a_r, 1)
                act.wait_ge(a_r, 2 * u + 1)
                nc.scalar.activation(rden[:], rden[:], ACT.Exp, scale=-1.0).then_inc(a_r, 1)

            def step(u, b, first=False, prev=True, more=True, far=True):
                i = b % 2
                if not first:
                    exps(u, i, 0)
                if prev:
                    reciprocal(u - 1)
                if more:
                    values(u + 1, (b + 1) % 4)
                if not first:
                    exps(u, i, 1)
                if far:
                    high_parts(u + 2, i)
                    high_keys(u + 2, i)
                if more:
                    max_rows(u + 1, 1 - i, 0)
                    max_rows(u + 1, 1 - i, 1)

            high_parts(0, 0)
            high_keys(0, 0)
            step(-1, 3, first=True, prev=False)
            for b in range(B):
                if b == 2:
                    rsqrt(1)
                step(b, b, prev=b > 0)
            with act.Fori(1, PAIRS - 1) as p:
                for b in range(B):
                    step(B * p + b, b)
            for b in range(B):
                step(B * (PAIRS - 1) + b, b, more=b < B - 1, far=b < B - 2)
            reciprocal(UNITS - 1)
            for n in range(G * B):
                b, g = n // G, n % G
                act.wait_ge(p_hid, n + 1)
                nc.scalar.activation(gT[:, g, b * T:(b + 1) * T], hbank[n % 3][:], ACT.Gelu,
                                     bias=bias_h[:, g:g + 1]).then_inc(a_hid, 1)

        @block.vector
        def _(dve):
            done = [0]

            def ordered(ins):
                done[0] += 1
                ins.then_inc(v_step, 1)
                dve.wait_ge(v_step, done[0])

            def statistics(k, src, tiles):
                for t in tiles:
                    if k == 0 and t % TT == 0:
                        dve.wait_ge(d_x[t // TT], 16)
                    last = nc.vector.bn_stats(stats[:, t, :], src[:, t, :])
                ordered(last)
                for t in tiles:
                    last = nc.vector.bn_aggr(mv[:, t, :], stats[:, t, :])
                ordered(last)

            def variance():
                nc.vector.tensor_scalar(nrm[:, 0, :], mv[:, :, 1], LN_EPS, None, ALU.add).then_inc(v_var, 1)

            def newton(k):
                var, r, t2 = nrm[:, 0, :], nrm[:, 2, :], nrm[:, 3, :]
                dve.wait_ge(a_std, k + 1)
                ordered(nc.vector.tensor_tensor(t2, r, r, ALU.mult))
                ordered(nc.vector.tensor_tensor(t2, t2, var, ALU.mult))
                ordered(nc.vector.tensor_scalar(t2, t2, -0.5, 1.5, ALU.mult, ALU.add))
                ordered(nc.vector.tensor_tensor(r, r, t2, ALU.mult))

            def low_folded(n):
                dve.wait_ge(a_fold, n + 2)
                o, r = FOLDS[n]
                nc.vector.tensor_tensor(w_all[:, r:r + 4, o + 1, :], mbank[n][:].rearrange("p (r c) -> p r c", c=P),
                                        w_all[:, r:r + 4, o, :].bitcast(F32), ALU.subtract).then_inc(v_fold, 1)

            def normal(dst, src, tiles):
                for t in tiles:
                    last = nc.vector.tensor_scalar(dst[:, t, :], src[:, t, :], mv[:, t, 0:1], nrm[:, 2, t:t + 1],
                                                   ALU.subtract, ALU.mult)
                return last

            statistics(0, x_sb, range(NT))
            variance()
            newton(0)
            for b in range(B):
                normal(xn, x_sb, range(b * TT, (b + 1) * TT)).then_inc(v_xn, 1)
            dve.wait_ge(a_fold, 1)
            nc.vector.scalar_tensor_tensor(out=w_all[:, :, 1, :], in0=wq_raw.rearrange("p (r c) -> p r c", c=P),
                                           scalar=SCALE, in1=w_all[:, :, 0, :].bitcast(F32), op0=ALU.mult,
                                           op1=ALU.subtract).then_inc(v_fold, 1)
            for n in range(4):
                low_folded(n)
            for b in range(B):
                c = slice(b * T, (b + 1) * T)
                dve.wait_ge(a_xnT, b + 1)
                nc.vector.tensor_tensor(xl[:, c], tbank[b][:], xh[:, c].bitcast(F32), ALU.subtract).then_inc(v_xl, 1)
            dve.wait_ge(p_rows, 1)
            nc.vector.tensor_copy(cols8[:].rearrange("p a e -> p (a e)"), be[:, 0:3 * E]).then_inc(v_cols, 1)

            def choose():
                dve.wait_ge(p_logit, 1)
                nc.vector.tensor_copy(bias_h[:], st_c[:, NT * E:NT * E + G])
                nc.vector.tensor_copy(logit[:].rearrange("p t e -> p (t e)"), st_c[:, 0:NT * E]).then_inc(v_logit, 1)
                dve.wait_ge(v_logit, 1)
                ordered(nc.vector.tensor_reduce(best[:, 0, :], logit[:], mybir.AxisListType.X, ALU.max))
                ordered(nc.vector.tensor_tensor(pick[:], logit[:], best[:, 0, :].unsqueeze(2).to_broadcast([P, NT, E]),
                                                ALU.is_ge))
                ordered(nc.vector.tensor_tensor(pick[:], pick[:], order[:].unsqueeze(1).to_broadcast([P, NT, E]),
                                                ALU.mult))
                ordered(nc.vector.tensor_reduce(best[:, 1, :], pick[:], mybir.AxisListType.X, ALU.max))
                nc.vector.tensor_tensor(pick[:], pick[:], best[:, 1, :].unsqueeze(2).to_broadcast([P, NT, E]),
                                        ALU.is_ge).then_inc(v_pick, 1)

            def low_parts(u, i):
                dve.wait_ge(a_q, u + 1)
                for h in range(2):
                    own = slice(0, DH) if h == 0 else slice(DH, P)
                    other = slice(DH, P) if h == 0 else slice(0, DH)
                    last = nc.vector.tensor_tensor(QS[i][h][other, :], bq[own, :], QS[i][h][own, :].bitcast(F32),
                                            ALU.subtract)
                last.then_inc(v_q, 1)

            def low_keys(u, i):
                dve.wait_ge(a_k, u + 1)
                for h in range(2):
                    own = slice(0, DH) if h == 0 else slice(DH, P)
                    last = nc.vector.tensor_tensor(KL[i][h][own, :], bk[own, :], KD[i][h][own, :].bitcast(F32),
                                                   ALU.subtract)
                last.then_inc(v_k, 1)

            def maxima(u, h):
                base = 3 * (2 * u + h)
                for n, parts in enumerate((((bd, 0, 3),), ((be, 0, 2), (be, 384, 0)), ((bd, 0, 1),))):
                    dve.wait_ge(s_x, base + n + 1)
                    dve.sem_inc(v_turn, 1)
                    for src, c0, j in parts:
                        w = P * (j + 1)
                        last = nc.vector.tensor_tensor_reduce(
                            out=src[:, c0:c0 + w], in0=src[:, c0:c0 + w], in1=neg_qk[:, 512 - w:512], scale=1.0,
                            scalar=-3.0e38, op0=ALU.add, op1=ALU.max, accum_out=mx[h][:, j:j + 1])
                    last.then_inc(v_x, 1)

            def invert(u):
                dve.wait_ge(a_r, 2 * u + 2)
                if not isinstance(u, int) or u > 0:
                    dve.wait_ge(v_n, u)
                nc.vector.tensor_tensor(scratch[:], bk[:], rden[:], ALU.mult).then_inc(v_r, 1)
                dve.wait_ge(v_r, u + 1)
                nc.vector.scalar_tensor_tensor(out=scratch[:], in0=scratch[:], scalar=2.0, in1=rden[:],
                                               op0=ALU.subtract, op1=ALU.mult).then_inc(v_r2, 1)

            def normalise(u, p, b):
                dve.wait_ge(v_r2, u + 1)
                dve.wait_ge(s_y, u + 1)
                nc.vector.scalar_tensor_tensor(out=yT[:, p, b * T:(b + 1) * T], in0=by[:], scalar=-1.0,
                                               in1=scratch[:], op0=ALU.mult, op1=ALU.mult).then_inc(v_n, 1)

            def step(u, p, b, first=False, norm=True, more=True, far=True):
                i = b % 2
                if norm:
                    invert(u - 1)
                if more:
                    maxima(u + 1, 0)
                    maxima(u + 1, 1)
                if far:
                    low_parts(u + 2, i)
                    low_keys(u + 2, i)
                if norm:
                    normalise(u - 1, p if b else p - 1, (b - 1) % B)

            low_parts(0, 0)
            low_keys(0, 0)
            step(-1, 0, 3, norm=False)
            choose()
            for b in range(B):
                step(b, 0, b, norm=b > 0)
                if b < 2:
                    statistics(1, xn, range(b * NT // 2, (b + 1) * NT // 2))
                if b == 1:
                    variance()
                if b == 2:
                    newton(1)
                if b >= 2:
                    normal(xhat, xn, range((b - 2) * NT // 2, (b - 1) * NT // 2)).then_inc(v_xhat, 1)
            with dve.Fori(1, PAIRS - 1) as p:
                for b in range(B):
                    step(B * p + b, p, b)
            for b in range(B):
                step(B * (PAIRS - 1) + b, PAIRS - 1, b, more=b < B - 1, far=b < B - 2)
            for b in range(B):
                dve.wait_ge(p_xhatT, b + 1)
                nc.vector.tensor_copy(xhatT[:, b * T:(b + 1) * T], (hbank + ebank)[b][:]).then_inc(v_xhatT, 1)
            for b in range(B):
                dve.wait_ge(p_maskT, b + 1)
                nc.vector.tensor_copy(maskT[:, b * T:(b + 1) * T], (hbank + ebank)[b][0:E, :]).then_inc(v_maskT, 1)
            invert(UNITS - 1)
            normalise(UNITS - 1, PAIRS - 1, B - 1)
            for n in range(G * B):
                b, g = n // G, n % G
                dve.wait_ge(p_exp, n + 1)
                dve.wait_ge(a_hid, n + 1)
                c = gT[:, g, b * T:(b + 1) * T]
                nc.vector.tensor_tensor(c, ebank[n % 2][:], c, ALU.mult).then_inc(v_gm, 1)
            for b in range(B):
                dve.wait_ge(s_o, b + 1)
                if b >= 2:
                    dve.wait_ge(d_out[b % 2], 16)
                dve.wait_ge(d_xa[b], 16)
                nc.vector.tensor_tensor(res[b % 2][:], obank[b % 2][:], x_again[b], ALU.add).then_inc(v_o, 1)

        @block.tensor
        def _(pe):
            mm = nc.tensor.matmul
            pe.wait_ge(g_const, 1)
            pe.wait_ge(d_wd, 16)
            nc.tensor.transpose(by[:, 0:P], wd, ident[:]).then_inc(p_wdT, 1)
            pe.wait_ge(a_wdT, 1)
            pe.wait_ge(d_kv, 16)
            for n in range(4):
                o, r = FOLDS[n]
                c0 = (o - 2) // 2 * HD + r * P
                mm(mbank[n][:], wdT, kv_up[:, c0:c0 + 512], start=True, stop=True).then_inc(p_fold, 1)
            for b in range(B):
                pe.wait_ge(v_xn, b + 1)
                for j in range(TT):
                    last = nc.tensor.transpose(tbank[b][:, j * P:(j + 1) * P], xn[:, b * TT + j, :], ident[:])
                last.then_inc(p_xnT, 1)
            pe.wait_ge(v_fold, 5)
            pe.wait_ge(d_small, 16 * 5)
            for a in range(3):
                last = nc.tensor.transpose(be[:, a * E:(a + 1) * E], rows8[:, a, :], ident[0:E, 0:E])
            last.then_inc(p_rows, 1)

            def logits():
                pe.wait_ge(v_cols, 1)
                pe.wait_ge(a_xnT, B)
                pe.wait_ge(v_xl, B)
                for t in range(NT):
                    mm(st_c[:, t * E:(t + 1) * E], xnT[:, t * P:(t + 1) * P], cols8[:, 0, :], start=True, stop=True)
                pe.wait_ge(g_w1, 2)
                for g in range(G):
                    c = st_c[:, NT * E + g:NT * E + g + 1]
                    mm(c, w1b.rearrange("p e h -> p (e h)")[:, g * P:(g + 1) * P], ones[:, 0:1], start=True, stop=False)
                    last = mm(c, b1_rows[:], ident[0:G, g:g + 1], start=False, stop=True)
                last.then_inc(p_logit, 1)

            def project_q(p, b):
                c = slice(b * T, (b + 1) * T)
                for n, (w, xx) in enumerate(((0, xh), (0, xl), (1, xh))):
                    last = mm(bq[:], w_qk[:, w, :], xx[:, c], start=n == 0, stop=n == 2)
                last.then_inc(s_q, 1)

            def project_k(p, b):
                c = slice(b * T, (b + 1) * T)
                for n, (w, xx) in enumerate(((2, xh), (2, xl), (3, xh))):
                    last = mm(bk[:], w_qk[:, w, :], xx[:, c], start=n == 0, stop=n == 2)
                last.then_inc(s_k, 1)

            def project_v(b):
                for j in range(TT):
                    c = slice(b * T + j * P, b * T + (j + 1) * P)
                    for n, (xx, w) in enumerate(((xh, 0), (xh, 1), (xl, 0))):
                        last = mm(by[:, j * P:(j + 1) * P], xx[:, c], w_v[:, w, :], start=n == 0, stop=n == 2)
                last.then_inc(s_v, 1)

            def score_piece(i, h, dst, parts):
                for c0, j in parts:
                    w = T - P * j
                    k = slice(j * P, (j + 1) * P)
                    mm(dst[:, c0:c0 + w], KD[i][h][:, k], QS[i][h][:, T - w:T], start=True, stop=False)
                    last = mm(dst[:, c0:c0 + w], KL[i][h][:, k], QM[i][h][:, T - w:T], start=False, stop=True)
                last.then_inc(s_st, 1)

            def all_scores(u, i, h):
                pe.wait_ge(a_m, 2 * u + h + 1)
                for n, (dst, parts) in enumerate(((st_a, ((0, 0),)), (st_b, ((0, 1), (384, 3))), (st_c, ((0, 2),)))):
                    s = 3 * (2 * u + h) + n - 2
                    if not isinstance(s, int) or s > 0:
                        pe.wait_ge(a_e, s)
                    score_piece(i, h, dst, parts)

            def max_piece(i, h, dst, parts):
                for c0, j in parts:
                    w = P * (j + 1)
                    last = mm(dst[:, c0:c0 + w], QS[i][h][:, j * P:(j + 1) * P], KD[i][h][:, 0:w], start=True, stop=True)
                last.then_inc(s_x, 1)

            def pv(b, j):
                i, s = b % 2, b % 4
                w = T - P * j
                c0 = (0, 512, 1024, 896)[j]
                for h in range(2):
                    last = mm(by[h * DH:(h + 1) * DH, P * j:T], VS[s][:, j * P + h * DH:j * P + (h + 1) * DH],
                              PR[i][h][:, c0:c0 + w], start=j == 0, stop=j == TT - 1)
                if j == TT - 1:
                    last.then_inc(s_y, 1)

            def denominators(b):
                i = b % 2
                for h in range(2):
                    mm(bk[h * DH:(h + 1) * DH, 0:P], ones[:], PR[i][h][:, 0:P], start=True, stop=True)
                    last = mm(bk[h * DH:(h + 1) * DH, P:T], ones[:], PS[i][h][:], start=True, stop=True)
                last.then_inc(s_l, 1)

            def spread_max(h):
                mm((be, bd)[h][:], ones_r[:], DG[h][:].rearrange("p t c -> p (t c)"), start=True, stop=True).then_inc(s_m, 1)

            def step(u, p, b, first=False, prev=True, more=True, far=True):
                i = b % 2
                nb, fb, pb = (b + 1) % B, (b + 2) % B, (b - 1) % B
                np_ = p if b < B - 1 else p + 1
                fp = p if b < B - 2 else p + 1
                if not first:
                    all_scores(u, i, 0)
                if prev:
                    if far or more:
                        pe.wait_ge(v_k, u + 2)
                    else:
                        pe.wait_ge(v_r, u - 1)
                    pe.wait_ge(g_s, 2 * u)
                    denominators(pb)
                if more:
                    pe.wait_ge(d_wv, 16 * (np_ + 1))
                    if prev and not (isinstance(u, int) and u < 2):
                        pe.wait_ge(v_n, u - 1)
                    project_v(nb)
                if not first:
                    all_scores(u, i, 1)
                if more:
                    pe.wait_ge(v_q, u + 2)
                    pe.wait_ge(v_k, u + 2)
                    if not first:
                        pe.wait_ge(a_m, 2 * u + 2)
                    max_piece(1 - i, 0, bd, ((0, 3),))
                    max_piece(1 - i, 0, be, ((0, 2), (384, 0)))
                if far:
                    pe.wait_ge(d_wqk, 16 * (fp + 1))
                    pe.wait_ge(v_q, u + 2)
                    project_q(fp, fb)
                if more:
                    pe.wait_ge(v_x, 6 * (u + 1) + 1)
                    max_piece(1 - i, 0, bd, ((0, 1),))
                if far:
                    if prev:
                        pe.wait_ge(v_r, u)
                    project_k(fp, fb)
                if more:
                    pe.wait_ge(v_x, 6 * (u + 1) + 3)
                    max_piece(1 - i, 1, bd, ((0, 3),))
                    max_piece(1 - i, 1, be, ((0, 2), (384, 0)))
                if prev:
                    if more:
                        pe.wait_ge(a_v, u + 2)
                    else:
                        pe.wait_ge(v_n, u - 1)
                    pe.wait_ge(g_s, 2 * u)
                    pv(pb, 0)
                if more:
                    pe.wait_ge(v_x, 6 * (u + 1) + 4)
                    max_piece(1 - i, 1, bd, ((0, 1),))
                if prev:
                    pv(pb, 1)
                if first:
                    logits()
                if more:
                    pe.wait_ge(g_d, 2 * (u + 1) + 1)
                    pe.wait_ge(v_x, 6 * (u + 1) + 5)
                    spread_max(0)
                if prev:
                    pv(pb, 2)
                    pv(pb, 3)
                if more:
                    pe.wait_ge(g_d, 2 * (u + 1) + 2)
                    pe.wait_ge(v_x, 6 * (u + 1) + 6)
                    spread_max(1)

            pe.wait_ge(g_const, 4)
            pe.wait_ge(d_wqk, 16)
            pe.wait_ge(v_xl, 1)
            project_q(0, 0)
            project_k(0, 0)
            pe.wait_ge(v_cols, 1)
            pe.wait_ge(v_xl, B)
            step(-1, -1, B - 1, first=True, prev=False)
            pe.wait_ge(v_logit, 1)
            for b in range(B):
                step(b, 0, b, prev=b > 0)
            with pe.Fori(1, PAIRS - 1) as p:
                for b in range(B):
                    step(B * p + b, p, b)
            for b in range(B):
                step(B * (PAIRS - 1) + b, PAIRS - 1, b, more=b < B - 1, far=b < B - 2)
            tb = hbank + ebank
            pe.wait_ge(v_xhat, 2)
            for b in range(B):
                if b == 3:
                    pe.wait_ge(a_e, 6 * UNITS - 2)
                for j in range(TT):
                    last = nc.tensor.transpose(tb[b][:, j * P:(j + 1) * P], xhat[:, b * TT + j, :], ident[:])
                last.then_inc(p_xhatT, 1)
            pe.wait_ge(v_pick, 1)
            for b in range(B):
                pe.wait_ge(v_xhatT, b + 1)
                for j in range(TT):
                    last = nc.tensor.transpose(tb[b][0:E, j * P:(j + 1) * P], pick[:, b * TT + j, :], ident[:])
                last.then_inc(p_maskT, 1)

            def hidden(n):
                b, g = n // G, n % G
                if n >= 3:
                    pe.wait_ge(a_hid, n - 2)
                mm(hbank[n % 3][:], w1s[:].rearrange("p e h -> p (e h)")[:, g * P:(g + 1) * P],
                   xhatT[:, b * T:(b + 1) * T], start=True, stop=True).then_inc(p_hid, 1)

            for n in range(3):
                pe.wait_ge(v_maskT, n + 1)
                hidden(n)
            pe.wait_ge(g_s, 2 * UNITS)
            pe.wait_ge(v_r, UNITS - 1)
            denominators(B - 1)
            pe.wait_ge(v_n, UNITS - 1)
            for j in range(TT):
                pv(B - 1, j)
            pe.wait_ge(v_maskT, B)
            for n in range(G * B):
                b, g = n // G, n % G
                if n >= 3:
                    hidden(n)
                if n >= 2:
                    pe.wait_ge(v_gm, n - 1)
                mm(ebank[n % 2][:], expand[:, g * P:(g + 1) * P], maskT[:, b * T:(b + 1) * T],
                   start=True, stop=True).then_inc(p_exp, 1)

            pe.wait_ge(d_late, 16 * 3)
            pe.wait_ge(v_n, UNITS)
            pe.wait_ge(v_r, UNITS)
            for b in range(B):
                if b >= 2:
                    pe.wait_ge(v_o, b - 1)
                for j in range(TT):
                    c = slice(b * T + j * P, b * T + (j + 1) * P)
                    dst = obank[b % 2][:, j * P:(j + 1) * P]
                    for r in range(PAIRS):
                        mm(dst, yT[:, r, c], wout_sb[:, r, :], start=r == 0, stop=False)
                    mm(dst, maskT[:, c].bitcast(F32), b2_sb[:], start=False, stop=False)
                    if j == 0:
                        pe.wait_ge(v_gm, G * (b + 1))
                    for g in range(G):
                        last = mm(dst, gT[:, g, c], w2_sb[:, g, :], start=False, stop=g == G - 1)
                last.then_inc(s_o, 1)


_INS = ["L0_attn_x", "L0_attn_w_kv_down", "L0_attn_w_kv_up", "L0_attn_w_q", "L0_attn_w_out", "L0_ffn_Wg",
        "L0_ffn_ln_scale", "L0_ffn_ln_bias", "L0_ffn_W1", "L0_ffn_b1", "L0_ffn_W2", "L0_ffn_b2"]


def kernel(**inputs):
    import numpy as _np
    import concourse.bacc as _bacc
    from concourse import mybir as _mybir
    from concourse.bass_utils import run_bass_kernel_spmd as _run

    nc = _bacc.Bacc("TRN2", target_bir_lowering=False, num_devices=1)
    arrays, args = {}, []
    for name in _INS:
        a = _np.ascontiguousarray(inputs[name])
        arrays[f"in_{name}_dram"] = a
        args.append(nc.dram_tensor(f"in_{name}_dram", a.shape, _mybir.dt.from_np(a.dtype), kind="ExternalInput").ap())
    shape = inputs["L0_attn_x"].shape
    dt = _mybir.dt.from_np(_np.dtype("float32"))
    args.append(nc.dram_tensor("out_0_dram", shape, dt, kind="ExternalOutput").ap())
    attention_and_experts(nc, *args)
    r = _run(nc, [arrays], core_ids=[0])
    return r.results[0]["out_0_dram"]
```

```python
import concourse.bass as bass
from concourse import mybir
from contextlib import ExitStack

F32 = mybir.dt.float32
F32R = mybir.dt.float32r
ALU = mybir.AluOpType
ACT = mybir.ActivationFunctionType

P = 128
NEG = -1.0e30
LN_EPS = 1e-5


def attention_and_experts(nc, x, w_kv_down, w_kv_up, w_q, w_out, wg, ln_scale, ln_bias, w1, b1, w2, b2, out):
    B, T, C = x.shape
    HD = w_q.shape[1]
    E, _, HID = w1.shape
    DH = 64
    PAIRS = HD // P
    TT = T // P
    NT = B * TT
    TOK = B * T
    G = E * HID // P
    UNITS = PAIRS * B
    ROUND = 2 * B
    ROUNDS = PAIRS // 2
    HEAD = 6
    SCALE = float(DH) ** -0.5
    assert C == P and T == 512 and w_kv_down.shape[1] == P and B == 4

    with ExitStack() as ctx:
        def sb(name, shape, dt=F32):
            return ctx.enter_context(nc.sbuf_tensor(name, shape, dt))

        def bank(name):
            return ctx.enter_context(nc.psum_tensor(name, [P, 512], F32))

        def sem(name):
            return ctx.enter_context(nc.semaphore(name))

        yT = sb("yT", [P, PAIRS, TOK])
        xn = yT[:, 7, :].rearrange("p (t c) -> p t c", c=C)
        xnT = yT[:, 5, :]
        kv_up = yT[:, 3, :]
        wq_raw = yT[:, 2, 0:HD]
        w1_sb, w1b = (yT[:, 2, HD + n * E * HID:HD + (n + 1) * E * HID].rearrange("p (e h) -> p e h", e=E)
                      for n in range(2))
        x_sb = yT[:, 1, :].rearrange("p (t c) -> p t c", c=C)
        wd, wdT = yT[:, 2, TOK - 2 * P:TOK - P], yT[:, 2, TOK - P:TOK]
        xh = sb("xh", [P, TOK], F32R)
        xl = sb("xl", [P, TOK], F32R)
        w_qk = sb("w_qk", [P, 2, 4, P], F32R)
        w_v = sb("w_v", [P, 2, 2, P], F32R)
        w_later = sb("w_later", [P, PAIRS - 2, 6, P], F32R)
        xhat = sb("xhat", [P, NT, C])
        xhatT = sb("xhatT", [P, TOK])
        w1s = sb("w1s", [P, E, HID])
        w2_sb = sb("w2_sb", [P, G, C])
        b2_sb = sb("b2_sb", [E, C])
        rows8 = sb("rows8", [E, 3, C])
        cols8 = sb("cols8", [P, 3, E])
        b1_rows = sb("b1_rows", [G, P])
        bias_h = sb("bias_h", [P, G])
        ident = sb("ident", [P, P])
        neg_qk = sb("neg_qk", [P, 512])
        ones = sb("ones", [P, DH])
        ones_r = sb("ones_r", [P, P], F32R)
        expand = sb("expand", [E, E * HID], F32R)
        order = sb("order", [P, E])
        stats = sb("stats", [P, NT, 6])
        mv = sb("mv", [P, NT, 2])
        nrm = sb("nrm", [P, 4, NT])
        logit = sb("logit", [P, NT, E])
        pick = sb("pick", [P, NT, E])
        best = sb("best", [P, 2, NT])
        QSM = [[sb(f"QSM{i}{h}", [P, 2, 512], F32R) for h in range(2)] for i in range(2)]
        QS = [[q[:, 0, :] for q in row] for row in QSM]
        QM = [[q[:, 1, :] for q in row] for row in QSM]
        KD = [[sb(f"KD{i}{h}", [P, 512], F32R) for h in range(2)] for i in range(2)]
        KL = [[sb(f"KL{i}{h}", [P, 512], F32R) for h in range(2)] for i in range(2)]
        PR = [[sb(f"PR{i}{h}", [P, 1280]) for h in range(2)] for i in range(2)]
        PS = [[sb(f"PS{i}{h}", [P, 384]) for h in range(2)] for i in range(2)]
        VS = [sb(f"VS{i}", [P, TT, 2 * P]) for i in range(2)]
        DG = [sb(f"DG{h}", [P, TT, P], F32R) for h in range(2)]
        mx = [sb(f"mx{h}", [P, TT]) for h in range(2)]
        scratch = sb("scratch", [P, 512])
        rden = sb("rden", [P, 512])
        w_free = w_later[:].bitcast(F32).rearrange("p r w c -> p (r w c)")
        wout_sb = w_free[:, 0:PAIRS * C]
        vs0, vs1 = (v[:].rearrange("p t c -> p (t c)") for v in VS)
        x_again = [PR[0][0][:, 0:512], PR[0][0][:, 512:1024], vs0[:, 0:512], vs0[:, 512:1024]]
        outT = [PR[1][0][:, 0:512], PR[1][0][:, 512:1024]]
        res = [vs1[:, 0:512], scratch[:]]
        maskT = xl[0:E, :]
        b2_parts = (xh[0:E, PAIRS * C:(PAIRS + 1) * C], xh[0:E, (PAIRS + 1) * C:(PAIRS + 2) * C])
        wout_parts = (xh[:, 0:PAIRS * C], w_qk[:].rearrange("p q w c -> p (q w c)"))
        w2_parts = (w_v[:, 0, :, :], w_v[:, 1, :, :])
        BLOCKS = PAIRS + G
        EARLY = 2
        RING = [(q[:, 0, :], q[:, 1, :]) for q in QSM[0]] + [(KD[0][h][:], KL[0][h][:]) for h in range(2)]
        RING += [(q[:, 0, :], q[:, 1, :]) for q in QSM[1]] + [(KD[1][h][:], KL[1][h][:]) for h in range(2)]
        gT = w_free[:, 0:G * TOK].rearrange("p (g t) -> p g t", g=G)

        st_a, st_b, st_c = bank("st_a"), bank("st_b"), bank("st_c")
        bd, be = bank("bd"), bank("be")
        bq, bk = bank("bq"), bank("bk")
        by = bank("by")

        d_x = [sem(f"d_x{b}") for b in range(B)]
        d_wd = sem("d_wd")
        d_kv = [sem(f"d_kv{n}") for n in range(4)]
        d_wq = sem("d_wq")
        d_small = sem("d_small")
        d_late = sem("d_late")
        d_xa = [sem(f"d_xa{b}") for b in range(B)]
        d_wqk = sem("d_wqk")
        d_wv = sem("d_wv")
        d_out = [sem(f"d_out{i}") for i in range(2)]
        g_const = sem("g_const")
        g_step, v_step = sem("g_step"), sem("v_step")
        p_wdT, a_wdT = sem("p_wdT"), sem("a_wdT")
        p_fold, a_fold, v_fold = sem("p_fold"), sem("a_fold"), sem("v_fold")
        v_var, a_log, a_std = sem("v_var"), sem("a_log"), sem("a_std")
        v_xn, p_xnT, a_xnT, v_xl = sem("v_xn"), sem("p_xnT"), sem("a_xnT"), sem("v_xl")
        v_xhat = sem("v_xhat")
        p_rows, v_cols, g_w1 = sem("p_rows"), sem("v_cols"), sem("g_w1")
        p_logit, v_logit, v_pick = sem("p_logit"), sem("v_logit"), sem("v_pick")
        s_q, s_k, s_v = sem("s_q"), sem("s_k"), sem("s_v")
        a_q, a_k, a_v = sem("a_q"), sem("a_k"), sem("a_v")
        v_q, v_k = sem("v_q"), sem("v_k")
        s_x, v_x = sem("s_x"), sem("v_x")
        v_turn, g_turn = sem("v_turn"), sem("g_turn")
        g_d, s_m, a_m = sem("g_d"), sem("s_m"), sem("a_m")
        s_st, a_e = sem("s_st"), sem("a_e")
        g_s1 = sem("g_s1")
        g_s = sem("g_s")
        s_y, s_l = sem("s_y"), sem("s_l")
        a_r, v_r, v_r2 = sem("a_r"), sem("v_r"), sem("v_r2")
        v_n = sem("v_n")
        p_xhatT, a_xhatT = sem("p_xhatT"), sem("a_xhatT")
        p_maskT, v_maskT = sem("p_maskT"), sem("v_maskT")
        p_hid, a_hid = sem("p_hid"), sem("a_hid")
        p_exp, v_gm = sem("p_exp"), sem("v_gm")
        a_w, v_w = sem("a_w"), sem("v_w")
        a_hi, v_lo, g_lo = sem("a_hi"), sem("v_lo"), sem("g_lo")
        s_used = sem("s_used")
        a_oT, s_o, v_o = sem("a_oT"), sem("s_o"), sem("v_o")

        x_v = x.rearrange("b (j p) c -> p (b j) c", p=P)
        out_v = out.rearrange("b (j p) c -> p (b j) c", p=P)

        PIECES = ((bd, ((0, 0, 3),)), (be, ((0, 0, 2), (0, 384, 0))), (bd, ((0, 0, 1), (1, 256, 1))),
                  (be, ((1, 0, 3),)), (bd, ((1, 0, 2), (1, 384, 0))))

        block = ctx.enter_context(nc.Block())

        tbank = [by, st_a, st_b, st_c]
        mbank = [bq, bk, bd, be]
        first_k, first_v = (w_qk[:, :, 2, :], w_qk[:, :, 3, :], 0, 256), (w_v[:, :, 0, :], w_v[:, :, 1, :], 0, 256)
        FOLDS = ((0, (first_k, (w_later[:, 0:2, 2, :], w_later[:, 0:2, 3, :], 256, 512))),
                 (HD, (first_v, (w_later[:, 0:2, 4, :], w_later[:, 0:2, 5, :], 256, 512))),
                 (512, ((w_later[:, 2:6, 2, :], w_later[:, 2:6, 3, :], 0, 512),)),
                 (HD + 512, ((w_later[:, 2:6, 4, :], w_later[:, 2:6, 5, :], 0, 512),)))
        hbank = [bd, be, bq]
        ebank = [st_a, st_b]
        obank = [st_c, bk]
        rbank = [by, bd]
        PARTS = [(b, 0, TT, rbank[b % 2]) for b in range(B - 1)]
        PARTS += [(B - 1, 0, TT // 2, rbank[1]), (B - 1, TT // 2, TT, be)]

        def source(n):
            b, r = n // BLOCKS, n % BLOCKS
            c = slice(b * T, (b + 1) * T)
            return yT[:, r, c] if r < PAIRS else gT[:, r - PAIRS, c]

        def by_pool(n):
            return n % 4 == 3

        @block.sync
        def _(sp):
            for b in range(B):
                sp.dma_start(x_sb[:, b * TT:(b + 1) * TT, :], x_v[:, b * TT:(b + 1) * TT, :]).then_inc(d_x[b], 16)
            sp.dma_start(kv_up[:, 0:HD // 2], w_kv_up[:, 0:HD // 2]).then_inc(d_kv[0], 16)
            sp.dma_start(kv_up[:, HD:HD * 3 // 2], w_kv_up[:, HD:HD * 3 // 2]).then_inc(d_kv[1], 16)
            sp.dma_start(wq_raw, w_q).then_inc(d_wq, 16)
            sp.dma_start(kv_up[:, HD // 2:HD], w_kv_up[:, HD // 2:HD]).then_inc(d_kv[2], 16)
            sp.dma_start(kv_up[:, HD * 3 // 2:2 * HD], w_kv_up[:, HD * 3 // 2:2 * HD]).then_inc(d_kv[3], 16)
            sp.dma_start(rows8[:, 0, :], wg).then_inc(d_small, 16)
            sp.dma_start(rows8[:, 1, :], ln_scale).then_inc(d_small, 16)
            sp.dma_start(rows8[:, 2, :], ln_bias).then_inc(d_small, 16)
            sp.dma_start(b1_rows[:], b1.rearrange("(g e) h -> g (e h)", g=G)).then_inc(d_small, 16)
            sp.dma_start(w1_sb, w1.rearrange("e d h -> d e h")).then_inc(d_small, 16)
            sp.dma_start(w2_sb[:], w2.rearrange("(g e) h c -> (e h) g c", g=G)).then_inc(d_late, 16)
            sp.dma_start(b2_sb[:], b2).then_inc(d_late, 16)
            sp.wait_ge(v_fold, 6)
            with sp.Fori(1, ROUNDS) as r:
                sp.wait_ge(s_k, ROUND * r)
                later = w_later[:, bass.ds(2 * (r - 1), 2), :, :].bitcast(F32)
                sp.dma_start(w_qk[:].bitcast(F32), later[:, :, 0:4, :]).then_inc(d_wqk, 16)
                sp.wait_ge(s_v, ROUND * r)
                sp.dma_start(w_v[:].bitcast(F32), later[:, :, 4:6, :]).then_inc(d_wv, 16)
            sp.wait_ge(d_wqk, 16 * (ROUNDS - 1))
            sp.wait_ge(d_wv, 16 * (ROUNDS - 1))
            sp.dma_start(wout_sb.rearrange("p (r c) -> p r c", c=C),
                         w_out.rearrange("(r p) c -> p r c", p=P)).then_inc(d_late, 16)
            sp.wait_ge(s_l, UNITS - 1)
            sp.wait_ge(s_y, UNITS - 1)
            for b in range(B):
                sp.dma_start(x_again[b].rearrange("p (t c) -> p t c", c=C),
                             x_v[:, b * TT:(b + 1) * TT, :]).then_inc(d_xa[b], 16)
            for n, (b, t0, t1, _) in enumerate(PARTS):
                sp.wait_ge(v_o, n + 1)
                sp.dma_start(out_v[:, b * TT + t0:b * TT + t1, :],
                             res[b % 2][:, t0 * C:t1 * C].rearrange("p (t c) -> p t c", c=C)).then_inc(d_out[b % 2], 16)
            for i in range(2):
                sp.wait_ge(d_out[i], 16 * sum(b % 2 == i for b, _, _, _ in PARTS))

        @block.gpsimd
        def _(pool):
            done = [0]

            def ordered(ins):
                done[0] += 1
                ins.then_inc(g_step, 1)
                pool.wait_ge(g_step, done[0])

            ordered(nc.gpsimd.memset(ident[:], 0.0))
            nc.gpsimd.affine_select(out=ident[:], in_=ident[:], compare_op=ALU.not_equal, fill=1.0, base=0,
                                    pattern=[[-1, P]], channel_multiplier=1).then_inc(g_const, 1)
            ordered(nc.gpsimd.memset(neg_qk[:], 0.0))
            nc.gpsimd.affine_select(out=neg_qk[:, 384:512], in_=neg_qk[:, 384:512], compare_op=ALU.is_ge,
                                    fill=NEG, base=0, pattern=[[-1, P]], channel_multiplier=1).then_inc(g_const, 1)
            wide = scratch[0:E, 0:E * HID]
            ordered(nc.gpsimd.memset(wide, 0.0))
            ordered(nc.gpsimd.affine_select(out=wide.rearrange("e (f h) -> e f h", f=E),
                                            in_=wide.rearrange("e (f h) -> e f h", f=E),
                                            compare_op=ALU.not_equal, fill=1.0, base=0,
                                            pattern=[[-1, E], [0, HID]], channel_multiplier=1))
            nc.gpsimd.tensor_copy(expand[:], wide).then_inc(g_const, 1)
            nc.gpsimd.memset(ones[:], 1.0)
            nc.gpsimd.memset(ones_r[:].bitcast(F32), 1.0)
            for e in range(E):
                last = nc.gpsimd.memset(order[:, e:e + 1], float(E - e))
            ordered(last)
            for i in range(2):
                ordered(nc.gpsimd.memset(KL[i][0][DH:P, :].bitcast(F32), -1.0 / DH))
                last = nc.gpsimd.memset(KL[i][1][0:DH, :].bitcast(F32), -1.0 / DH)
                if i == 0:
                    ordered(last)
            last.then_inc(g_const, 1)
            pool.wait_ge(g_const, 4)
            pool.wait_ge(d_small, 16 * 5)
            pool.wait_ge(v_cols, 1)
            for dst, a in ((w1s[:], 1), (w1b, 2)):
                nc.gpsimd.tensor_tensor(dst, w1_sb, cols8[:, a, :].unsqueeze(2).to_broadcast([P, E, HID]),
                                        ALU.mult).then_inc(g_w1, 1)

            def diagonal(u, h, first, step, pieces):
                pool.wait_ge(v_x, 5 * u + pieces)
                tiles = slice(first, TT, step)
                nc.gpsimd.tensor_tensor(DG[h][:, tiles, :], ident[:].unsqueeze(1).to_broadcast([P, TT // step, P]),
                                        mx[h][:, tiles].unsqueeze(2).to_broadcast([P, TT // step, P]),
                                        ALU.mult).then_inc(g_d, 1)

            def causal(u, i, h):
                pr = PR[i][h]
                pool.wait_ge(a_e, 3 * (2 * u + h + 1))
                pool.sem_inc(g_turn, 1)
                for blocks in (pr[:, 0:1024].rearrange("p (k c) -> p k c", k=2)[:, :, 0:P],
                               pr[:, 896:1152].rearrange("p (k c) -> p k c", k=2)):
                    nc.gpsimd.affine_select(out=blocks, in_=blocks, compare_op=ALU.is_ge, fill=0.0, base=0,
                                            pattern=[[0, 2], [1, P]], channel_multiplier=-1).then_inc(g_s1, 1)
                pool.wait_ge(g_s1, 4 * (2 * u + h) + 2)
                nc.gpsimd.tensor_tensor(PS[i][h][:, 0:384], pr[:, 128:512], pr[:, 512:896], ALU.add).then_inc(g_s1, 1)

            def sums(u, i, h):
                pr, ps = PR[i][h], PS[i][h]
                base = 4 * (2 * u + h)
                pool.wait_ge(g_s1, base + 3)
                nc.gpsimd.tensor_tensor(ps[:, 128:384], ps[:, 128:384], pr[:, 1024:1280], ALU.add).then_inc(g_s1, 1)
                pool.wait_ge(g_s1, base + 4)
                nc.gpsimd.tensor_tensor(ps[:, 256:384], ps[:, 256:384], pr[:, 896:1024], ALU.add).then_inc(g_s, 1)

            def step(u, k, first=False, more=True):
                i = k % 2
                if not first:
                    causal(u, i, 0)
                    sums(u, i, 0)
                    causal(u, i, 1)
                if more:
                    diagonal(u + 1, 0, 0, 1, 3)
                    diagonal(u + 1, 1, 1, 2, 4)
                    diagonal(u + 1, 1, 0, 2, 5)
                if not first:
                    sums(u, i, 1)

            step(-1, 7, first=True)
            for k in range(HEAD):
                step(k, k)
            with pool.Fori(0, ROUNDS - 1) as r:
                for k in range(HEAD, HEAD + ROUND):
                    step(ROUND * r + k, k % ROUND)
            for k in range(HEAD, ROUND):
                step(UNITS - ROUND + k, k, more=k < ROUND - 1)

            for n in range(B * BLOCKS):
                if by_pool(n):
                    pool.wait_ge(a_hi, n + 1)
                    high, low = RING[n % len(RING)]
                    nc.gpsimd.tensor_tensor(low, source(n), high.bitcast(F32), ALU.subtract).then_inc(g_lo, 1)

        @block.scalar
        def _(act):
            nc.scalar.preload_act_table_set("natural_log_exp_and_others")
            act.dma_start(wd, w_kv_down).then_inc(d_wd, 16)
            act.wait_ge(p_wdT, 1)
            nc.scalar.activation(wdT, by[:, 0:P], ACT.Copy).then_inc(a_wdT, 1)

            def rsqrt(k):
                act.wait_ge(v_var, k + 1)
                nc.scalar.activation(nrm[:, 1, :], nrm[:, 0, :], ACT.Ln).then_inc(a_log, 1)
                act.wait_ge(a_log, k + 1)
                nc.scalar.activation(nrm[:, 2, :], nrm[:, 1, :], ACT.Exp, scale=-0.5).then_inc(a_std, 1)

            def high_folded(n):
                act.wait_ge(p_fold, n + 1)
                for high, _, c0, c1 in FOLDS[n][1]:
                    last = nc.scalar.activation(high, mbank[n][:, c0:c1].rearrange("p (r c) -> p r c", c=P), ACT.Copy)
                last.then_inc(a_fold, 1)

            def high_queries(dst, p0, p1):
                nc.scalar.activation(dst, wq_raw[:, p0 * P:p1 * P].rearrange("p (r c) -> p r c", c=P), ACT.Copy,
                                     scale=SCALE).then_inc(a_fold, 1)

            rsqrt(0)
            act.wait_ge(d_wq, 16)
            high_queries(w_qk[:, :, 0, :], 0, 2)
            high_folded(0)
            high_folded(1)
            for b in range(B):
                if b == 2:
                    high_folded(2)
                    high_folded(3)
                    high_queries(w_later[:, :, 0, :], 2, PAIRS)
                act.wait_ge(p_xnT, b + 1)
                nc.scalar.activation(xh[:, b * T:(b + 1) * T], tbank[b][:], ACT.Copy)
                nc.scalar.activation(xnT[:, b * T:(b + 1) * T], tbank[b][:], ACT.Copy).then_inc(a_xnT, 1)

            def high_parts(u, i):
                act.wait_ge(s_q, u + 1)
                for h, own in enumerate((slice(0, DH), slice(DH, P))):
                    last = nc.scalar.activation(QSM[i][h][own, :, :],
                                                bq[own, :].unsqueeze(1).to_broadcast([DH, 2, 512]), ACT.Copy)
                last.then_inc(a_q, 1)

            def high_keys(u, i):
                act.wait_ge(s_k, u + 1)
                nc.scalar.activation(KD[i][0][0:DH, :], bk[0:DH, :], ACT.Copy)
                nc.scalar.activation(KD[i][1][DH:P, :], bk[DH:P, :], ACT.Copy).then_inc(a_k, 1)

            def values(n, k):
                act.wait_ge(s_v, n + 1)
                j = TT // 2 * (k % 2)
                nc.scalar.activation(VS[k // 2 % 2][:, j:j + TT // 2, :], by[:].rearrange("p (t c) -> p t c", c=2 * P),
                                     ACT.Copy).then_inc(a_v, 1)

            def max_rows(u, i, h):
                act.wait_ge(s_m, 2 * u + h + 1)
                rows = slice(DH, P) if h == 0 else slice(0, DH)
                nc.scalar.activation(QM[i][h][rows, :], (be, bd)[h][rows, :], ACT.Copy).then_inc(a_m, 1)

            def exps(u, i, h):
                for n, (src, c0, w) in enumerate(((st_a, 0, 512), (st_b, 512, 512), (st_c, 1024, 256))):
                    act.wait_ge(s_st, 3 * (2 * u + h) + n + 1)
                    nc.scalar.activation(PR[i][h][:, c0:c0 + w], src[:, 0:w], ACT.Exp).then_inc(a_e, 1)

            def reciprocal(u):
                act.wait_ge(s_l, u + 1)
                if not isinstance(u, int) or u > 0:
                    act.wait_ge(v_r2, u)
                nc.scalar.activation(rden[:], bk[:], ACT.Ln).then_inc(a_r, 1)
                act.wait_ge(a_r, 2 * u + 1)
                nc.scalar.activation(rden[:], rden[:], ACT.Exp, scale=-1.0).then_inc(a_r, 1)

            def step(u, k, first=False, prev=True, more=True, far=True):
                i = k % 2
                if not first:
                    exps(u, i, 0)
                if prev:
                    reciprocal(u - 1)
                if not first:
                    exps(u, i, 1)
                if more:
                    values(u + 1, (k + 1) % ROUND)
                if far:
                    high_parts(u + 2, i)
                    high_keys(u + 2, i)
                if more:
                    max_rows(u + 1, 1 - i, 0)
                    max_rows(u + 1, 1 - i, 1)

            high_parts(0, 0)
            high_keys(0, 0)
            step(-1, 7, first=True, prev=False)
            for k in range(HEAD):
                if k == 3:
                    rsqrt(1)
                step(k, k, prev=k > 0)
            with act.Fori(0, ROUNDS - 1) as r:
                for k in range(HEAD, HEAD + ROUND):
                    step(ROUND * r + k, k % ROUND)
            for k in range(HEAD, ROUND):
                step(UNITS - ROUND + k, k, more=k < ROUND - 1, far=k < ROUND - 2)
            for b in range(B):
                act.wait_ge(p_xhatT, b + 1)
                nc.scalar.activation(xhatT[:, b * T:(b + 1) * T], (hbank + ebank)[b][:], ACT.Copy).then_inc(a_xhatT, 1)
            act.wait_ge(d_late, 16 * 3)
            nc.scalar.activation(wout_parts[0], wout_sb, ACT.Copy)
            nc.scalar.activation(w2_parts[0], w2_sb[:], ACT.Copy)
            nc.scalar.activation(b2_parts[0], b2_sb[:], ACT.Copy).then_inc(a_w, 1)

            def split_high(n):
                if n >= len(RING):
                    act.wait_ge(s_used, n - len(RING) + 1)
                b, r = n // BLOCKS, n % BLOCKS
                if r >= PAIRS:
                    act.wait_ge(v_gm, G * b + r - PAIRS + 1)
                else:
                    act.wait_ge(v_n, UNITS if n == B * BLOCKS - G - 1 else UNITS - 1)
                nc.scalar.activation(RING[n % len(RING)][0], source(n), ACT.Copy).then_inc(a_hi, 1)

            for n in range(len(RING)):
                split_high(n)
            reciprocal(UNITS - 1)
            act.wait_ge(v_w, 1)
            for n in range(G * B):
                b, g = n // G, n % G
                act.wait_ge(p_hid, n + 1)
                nc.scalar.activation(gT[:, g, b * T:(b + 1) * T], hbank[n % 3][:], ACT.Gelu,
                                     bias=bias_h[:, g:g + 1]).then_inc(a_hid, 1)
                if n >= 2:
                    split_high(len(RING) + n - 2)
            for n in range(len(RING) + G * B - 2, B * BLOCKS + 5):
                if n < B * BLOCKS:
                    split_high(n)
                if n % BLOCKS == 4 and n > BLOCKS:
                    act.wait_ge(s_used, n // BLOCKS * BLOCKS)
                    for b, t0, t1, _ in PARTS:
                        if b == n // BLOCKS - 1:
                            nc.scalar.activation(outT[b % 2][:, t0 * P:t1 * P], obank[b % 2][:, t0 * P:t1 * P],
                                                 ACT.Copy).then_inc(a_oT, 1)

        @block.vector
        def _(dve):
            done = [0]

            def ordered(ins):
                done[0] += 1
                ins.then_inc(v_step, 1)
                dve.wait_ge(v_step, done[0])

            def statistics(src, tiles):
                for t in tiles:
                    last = nc.vector.bn_stats(stats[:, t, :], src[:, t, :])
                return last

            def aggregate(tiles):
                for t in tiles:
                    last = nc.vector.bn_aggr(mv[:, t, :], stats[:, t, :])
                ordered(last)

            def variance():
                nc.vector.tensor_scalar(nrm[:, 0, :], mv[:, :, 1], LN_EPS, None, ALU.add).then_inc(v_var, 1)

            def newton(k):
                var, r, t2 = nrm[:, 0, :], nrm[:, 2, :], nrm[:, 3, :]
                dve.wait_ge(a_std, k + 1)
                ordered(nc.vector.tensor_tensor(t2, r, r, ALU.mult))
                ordered(nc.vector.tensor_tensor(t2, t2, var, ALU.mult))
                ordered(nc.vector.tensor_scalar(t2, t2, -0.5, 1.5, ALU.mult, ALU.add))
                ordered(nc.vector.tensor_tensor(r, r, t2, ALU.mult))

            def low_folded(n):
                dve.wait_ge(a_fold, n + 2)
                for high, low, c0, c1 in FOLDS[n][1]:
                    last = nc.vector.tensor_tensor(low, mbank[n][:, c0:c1].rearrange("p (r c) -> p r c", c=P),
                                                   high.bitcast(F32), ALU.subtract)
                last.then_inc(v_fold, 1)

            def normal(dst, src, tiles):
                for t in tiles:
                    last = nc.vector.tensor_scalar(dst[:, t, :], src[:, t, :], mv[:, t, 0:1], nrm[:, 2, t:t + 1],
                                                   ALU.subtract, ALU.mult)
                return last

            for b in range(B):
                dve.wait_ge(d_x[b], 16)
                last = statistics(x_sb, range(b * TT, (b + 1) * TT))
            ordered(last)
            aggregate(range(NT))
            variance()
            newton(0)
            for b in range(B):
                normal(xn, x_sb, range(b * TT, (b + 1) * TT)).then_inc(v_xn, 1)

            def low_queries(high, low, p0, p1):
                nc.vector.scalar_tensor_tensor(out=low, in0=wq_raw[:, p0 * P:p1 * P].rearrange("p (r c) -> p r c", c=P),
                                               scalar=SCALE, in1=high.bitcast(F32), op0=ALU.mult,
                                               op1=ALU.subtract).then_inc(v_fold, 1)

            def low_inputs(b):
                c = slice(b * T, (b + 1) * T)
                dve.wait_ge(a_xnT, b + 1)
                nc.vector.tensor_tensor(xl[:, c], tbank[b][:], xh[:, c].bitcast(F32), ALU.subtract).then_inc(v_xl, 1)

            dve.wait_ge(a_fold, 1)
            low_queries(w_qk[:, :, 0, :], w_qk[:, :, 1, :], 0, 2)
            low_folded(0)
            low_inputs(0)
            low_folded(1)
            low_inputs(1)
            low_folded(2)
            low_folded(3)

            def choose():
                dve.wait_ge(v_logit, 1)
                ordered(nc.vector.tensor_reduce(best[:, 0, :], logit[:], mybir.AxisListType.X, ALU.max))
                ordered(nc.vector.tensor_tensor(pick[:], logit[:], best[:, 0, :].unsqueeze(2).to_broadcast([P, NT, E]),
                                                ALU.is_ge))
                ordered(nc.vector.tensor_tensor(pick[:], pick[:], order[:].unsqueeze(1).to_broadcast([P, NT, E]),
                                                ALU.mult))
                ordered(nc.vector.tensor_reduce(best[:, 1, :], pick[:], mybir.AxisListType.X, ALU.max))
                nc.vector.tensor_tensor(pick[:], pick[:], best[:, 1, :].unsqueeze(2).to_broadcast([P, NT, E]),
                                        ALU.is_ge).then_inc(v_pick, 1)

            def low_parts(u, i):
                dve.wait_ge(a_q, u + 1)
                for h in range(2):
                    own = slice(0, DH) if h == 0 else slice(DH, P)
                    other = slice(DH, P) if h == 0 else slice(0, DH)
                    last = nc.vector.tensor_tensor(QS[i][h][other, :], bq[own, :], QS[i][h][own, :].bitcast(F32),
                                            ALU.subtract)
                last.then_inc(v_q, 1)

            def low_keys(u, i):
                dve.wait_ge(a_k, u + 1)
                nc.vector.tensor_copy(KD[i][0][DH:P, :], KD[i][0][0:DH, :])
                nc.vector.tensor_copy(KD[i][1][0:DH, :], KD[i][1][DH:P, :])
                for h in range(2):
                    own = slice(0, DH) if h == 0 else slice(DH, P)
                    last = nc.vector.tensor_tensor(KL[i][h][own, :], bk[own, :], KD[i][h][own, :].bitcast(F32),
                                                   ALU.subtract)
                last.then_inc(v_k, 1)

            def maxima(u, n):
                src, parts = PIECES[n]
                dve.wait_ge(s_x, 5 * u + n + 1)
                dve.sem_inc(v_turn, 1)
                for h, c0, j in parts:
                    w = P * (j + 1)
                    last = nc.vector.tensor_tensor_reduce(
                        out=src[:, c0:c0 + w], in0=src[:, c0:c0 + w], in1=neg_qk[:, 512 - w:512], scale=1.0,
                        scalar=-3.0e38, op0=ALU.add, op1=ALU.max, accum_out=mx[h][:, j:j + 1])
                last.then_inc(v_x, 1)

            def invert(u):
                dve.wait_ge(a_r, 2 * u + 2)
                if not isinstance(u, int) or u > 0:
                    dve.wait_ge(v_n, u)
                nc.vector.tensor_tensor(scratch[:], bk[:], rden[:], ALU.mult).then_inc(v_r, 1)

            def invert_more(u):
                dve.wait_ge(v_r, u + 1)
                nc.vector.scalar_tensor_tensor(out=scratch[:], in0=scratch[:], scalar=2.0, in1=rden[:],
                                               op0=ALU.subtract, op1=ALU.mult).then_inc(v_r2, 1)

            def normalise(u, p, b):
                dve.wait_ge(v_r2, u + 1)
                dve.wait_ge(s_y, u + 1)
                nc.vector.scalar_tensor_tensor(out=yT[:, p, b * T:(b + 1) * T], in0=by[:], scalar=-1.0,
                                               in1=scratch[:], op0=ALU.mult, op1=ALU.mult).then_inc(v_n, 1)

            def step(u, k, r, norm=True, more=True, far=True):
                i = k % 2
                if norm:
                    invert(u - 1)
                if more:
                    maxima(u + 1, 0)
                    maxima(u + 1, 1)
                    maxima(u + 1, 2)
                if norm:
                    invert_more(u - 1)
                if more:
                    maxima(u + 1, 3)
                    maxima(u + 1, 4)
                if far:
                    low_keys(u + 2, i)
                    low_parts(u + 2, i)
                if norm:
                    kp = (k - 1) % ROUND
                    normalise(u - 1, 2 * (r if k else r - 1) + kp % 2, kp // 2)

            dve.wait_ge(p_rows, 1)
            nc.vector.tensor_copy(cols8[:].rearrange("p a e -> p (a e)"), st_a[:, 0:3 * E]).then_inc(v_cols, 1)
            dve.wait_ge(v_xn, B)
            statistics(xn, range(0, TT))
            low_parts(0, 0)
            low_keys(0, 0)
            low_inputs(2)
            low_inputs(3)
            dve.wait_ge(p_logit, 1)
            nc.vector.tensor_copy(bias_h[:], st_a[:, 2 * P:2 * P + G])
            nc.vector.tensor_copy(logit[:].rearrange("p t e -> p (t e)"), st_a[:, P:P + NT * E]).then_inc(v_logit, 1)
            step(-1, 7, -1, norm=False)
            choose()
            statistics(xn, range(4, 8))
            for k in range(HEAD):
                step(k, k, 0, norm=k > 0)
                if k == 0:
                    dve.wait_ge(a_fold, 6)
                    low_queries(w_later[:, :, 0, :], w_later[:, :, 1, :], 2, PAIRS)
                    ordered(statistics(xn, range(8, 12)))
                if k == 1:
                    ordered(statistics(xn, range(12, 16)))
                    aggregate(range(NT))
                    variance()
                if k == 3:
                    newton(1)
                    normal(xhat, xn, range(0, 4)).then_inc(v_xhat, 1)
                if k == 4:
                    normal(xhat, xn, range(4, 10)).then_inc(v_xhat, 1)
                if k == 5:
                    normal(xhat, xn, range(10, 16)).then_inc(v_xhat, 1)
            with dve.Fori(0, ROUNDS - 1) as r:
                for k in range(HEAD, HEAD + ROUND):
                    step(ROUND * r + k, k % ROUND, r if k < ROUND else r + 1)
            for k in range(HEAD, ROUND):
                step(UNITS - ROUND + k, k, ROUNDS - 1, more=k < ROUND - 1, far=k < ROUND - 2)
            for b in range(B):
                dve.wait_ge(p_maskT, b + 1)
                nc.vector.tensor_copy(maskT[:, b * T:(b + 1) * T], (hbank + ebank)[b][0:E, :]).then_inc(v_maskT, 1)
            dve.wait_ge(a_w, 1)
            nc.vector.tensor_tensor(wout_parts[1], wout_sb, wout_parts[0].bitcast(F32), ALU.subtract)
            nc.vector.tensor_tensor(w2_parts[1], w2_sb[:], w2_parts[0].bitcast(F32), ALU.subtract)
            nc.vector.tensor_tensor(b2_parts[1], b2_sb[:], b2_parts[0].bitcast(F32), ALU.subtract).then_inc(v_w, 1)

            def split_low(n):
                if not by_pool(n):
                    dve.wait_ge(a_hi, n + 1)
                    high, low = RING[n % len(RING)]
                    nc.vector.tensor_tensor(low, source(n), high.bitcast(F32), ALU.subtract).then_inc(v_lo, 1)

            for n in range(4):
                split_low(n)
            invert(UNITS - 1)
            invert_more(UNITS - 1)
            normalise(UNITS - 1, PAIRS - 1, B - 1)
            for n in range(G * B):
                b, g = n // G, n % G
                dve.wait_ge(p_exp, n + 1)
                dve.wait_ge(a_hid, n + 1)
                c = gT[:, g, b * T:(b + 1) * T]
                nc.vector.tensor_tensor(c, ebank[n % 2][:], c, ALU.mult).then_inc(v_gm, 1)
                split_low(n + 4)
            for n in range(G * B + 4, B * BLOCKS + BLOCKS):
                if n < B * BLOCKS:
                    split_low(n)
                if n % BLOCKS == BLOCKS - 1 and n > BLOCKS:
                    for part, (b, t0, t1, src) in enumerate(PARTS):
                        if b == n // BLOCKS - 1:
                            dve.wait_ge(s_o, part + 1)
                            if b >= 2:
                                dve.wait_ge(d_out[b % 2], 16)
                            dve.wait_ge(d_xa[b], 16)
                            c = slice(t0 * C, t1 * C)
                            nc.vector.tensor_tensor(res[b % 2][:, c], src[:, c], x_again[b][:, c],
                                                    ALU.add).then_inc(v_o, 1)

        @block.tensor
        def _(pe):
            mm = nc.tensor.matmul
            pe.wait_ge(g_const, 1)
            pe.wait_ge(d_wd, 16)
            nc.tensor.transpose(by[:, 0:P], wd, ident[:]).then_inc(p_wdT, 1)
            pe.wait_ge(a_wdT, 1)
            for n in range(4):
                c0 = FOLDS[n][0]
                pe.wait_ge(d_kv[n], 16)
                mm(mbank[n][:], wdT, kv_up[:, c0:c0 + 512], start=True, stop=True).then_inc(p_fold, 1)
                if n > 0:
                    for b in ((0, 1), (2,), (3,))[n - 1]:
                        pe.wait_ge(v_xn, b + 1)
                        for j in range(TT):
                            last = nc.tensor.transpose(tbank[b][:, j * P:(j + 1) * P], xn[:, b * TT + j, :], ident[:])
                        last.then_inc(p_xnT, 1)

            def columns():
                pe.wait_ge(v_xl, 2)
                pe.wait_ge(d_small, 16 * 5)
                for a in range(3):
                    last = nc.tensor.transpose(st_a[:, a * E:(a + 1) * E], rows8[:, a, :], ident[0:E, 0:E])
                last.then_inc(p_rows, 1)

            def logits():
                pe.wait_ge(v_cols, 1)
                pe.wait_ge(a_xnT, B)
                for t in range(NT):
                    mm(st_a[:, P + t * E:P + (t + 1) * E], xnT[:, t * P:(t + 1) * P], cols8[:, 0, :],
                       start=True, stop=True)
                pe.wait_ge(g_w1, 2)
                for g in range(G):
                    c = st_a[:, 2 * P + g:2 * P + g + 1]
                    mm(c, w1b.rearrange("p e h -> p (e h)")[:, g * P:(g + 1) * P], ones[:, 0:1], start=True, stop=False)
                    last = mm(c, b1_rows[:], ident[0:G, g:g + 1], start=False, stop=True)
                last.then_inc(p_logit, 1)

            def project_q(k):
                c = slice(k // 2 * T, (k // 2 + 1) * T)
                for n, (w, xx) in enumerate(((0, xh), (0, xl), (1, xh))):
                    last = mm(bq[:], w_qk[:, k % 2, w, :], xx[:, c], start=n == 0, stop=n == 2)
                last.then_inc(s_q, 1)

            def project_k(k, n0=0, n1=3):
                c = slice(k // 2 * T, (k // 2 + 1) * T)
                for n, (w, xx) in list(enumerate(((2, xh), (2, xl), (3, xh))))[n0:n1]:
                    last = mm(bk[:], w_qk[:, k % 2, w, :], xx[:, c], start=n == 0, stop=n == 2)
                if n1 == 3:
                    last.then_inc(s_k, 1)

            def project_v(k):
                for t in range(TT // 2):
                    j = TT // 2 * (k % 2) + t
                    c = slice(k // 2 * T + j * P, k // 2 * T + (j + 1) * P)
                    for n, (xx, w) in enumerate(((xh, 0), (xh, 1), (xl, 0))):
                        last = mm(by[:, 2 * P * t:2 * P * (t + 1)].rearrange("p (q c) -> p q c", q=2), xx[:, c],
                                  w_v[:, :, w, :], start=n == 0, stop=n == 2)
                last.then_inc(s_v, 1)

            def score_piece(i, h, dst, parts):
                for c0, j in parts:
                    w = T - P * j
                    k = slice(j * P, (j + 1) * P)
                    mm(dst[:, c0:c0 + w], KD[i][h][:, k], QS[i][h][:, T - w:T], start=True, stop=False)
                    last = mm(dst[:, c0:c0 + w], KL[i][h][:, k], QM[i][h][:, T - w:T], start=False, stop=True)
                last.then_inc(s_st, 1)

            def all_scores(u, i, h):
                pe.wait_ge(a_m, 2 * u + h + 1)
                for n, (dst, parts) in enumerate(((st_a, ((0, 0),)), (st_b, ((0, 1), (384, 3))), (st_c, ((0, 2),)))):
                    s = 3 * (2 * u + h) + n - 2
                    if not isinstance(s, int) or s > 0:
                        pe.wait_ge(a_e, s)
                    score_piece(i, h, dst, parts)

            def max_piece(i, n):
                dst, parts = PIECES[n]
                for h, c0, j in parts:
                    w = P * (j + 1)
                    last = mm(dst[:, c0:c0 + w], QS[i][h][:, j * P:(j + 1) * P], KD[i][h][:, 0:w],
                              start=True, stop=True)
                last.then_inc(s_x, 1)

            def pv(k, j, c=0, n=T):
                i, s = k % 2, k // 2 % 2
                w = min(n, T - P * j - c)
                q0, c0 = P * j + c, (0, 512, 1024, 896)[j] + c
                for h in range(2):
                    last = mm(by[h * DH:(h + 1) * DH, q0:q0 + w], VS[s][:, j, i * P + h * DH:i * P + (h + 1) * DH],
                              PR[i][h][:, c0:c0 + w], start=j == 0 and c == 0, stop=j == TT - 1)
                if j == TT - 1:
                    last.then_inc(s_y, 1)

            def denominators(i):
                for h in range(2):
                    mm(bk[h * DH:(h + 1) * DH, 0:P], ones[:], PR[i][h][:, 0:P], start=True, stop=True)
                    last = mm(bk[h * DH:(h + 1) * DH, P:T], ones[:], PS[i][h][:], start=True, stop=True)
                last.then_inc(s_l, 1)

            def spread_max(h):
                mm((be, bd)[h][:], ones_r[:], DG[h][:].rearrange("p t c -> p (t c)"),
                   start=True, stop=True).then_inc(s_m, 1)

            def step(u, k, r, first=False, prev=True, more=True, far=True):
                i = k % 2
                kn, kf, kp = (k + 1) % ROUND, (k + 2) % ROUND, (k - 1) % ROUND
                rn = r if k < ROUND - 1 else r + 1
                rf = r if k < ROUND - 2 else r + 1
                if not first:
                    all_scores(u, i, 0)
                if prev:
                    if far or more:
                        pe.wait_ge(v_k, u + 2)
                    else:
                        pe.wait_ge(v_r, u - 1)
                    pe.wait_ge(g_s, 2 * u)
                    denominators(1 - i)
                if not first:
                    all_scores(u, i, 1)
                if more:
                    if kn == 0 and not first:
                        pe.wait_ge(d_wv, 16 * rn)
                    if prev and not (isinstance(u, int) and u < 2):
                        pe.wait_ge(v_n, u - 1)
                    project_v(kn)
                if first:
                    columns()
                    logits()
                    pe.wait_ge(v_fold, 5)
                if more:
                    pe.wait_ge(v_q, u + 2)
                    pe.wait_ge(v_k, u + 2)
                    if not first:
                        pe.wait_ge(a_m, 2 * u + 2)
                    max_piece(1 - i, 0)
                    max_piece(1 - i, 1)
                if far:
                    if kf == 0:
                        pe.wait_ge(d_wqk, 16 * rf)
                    pe.wait_ge(v_q, u + 2)
                    project_q(kf)
                    if prev:
                        pe.wait_ge(v_r, u)
                    project_k(kf, 0, 1)
                if more:
                    pe.wait_ge(v_x, 5 * (u + 1) + 1)
                    max_piece(1 - i, 2)
                if prev:
                    if more:
                        pe.wait_ge(a_v, u + 2)
                    else:
                        pe.wait_ge(v_n, u - 1)
                    pv(kp, 0, 0, T // 2)
                if more:
                    pe.wait_ge(v_x, 5 * (u + 1) + 2)
                    max_piece(1 - i, 3)
                if far:
                    project_k(kf, 1, 3)
                if more:
                    pe.wait_ge(v_x, 5 * (u + 1) + 3)
                    max_piece(1 - i, 4)
                if prev:
                    pv(kp, 0, T // 2, T // 2)
                    pv(kp, 1, P, 2 * P)
                    pv(kp, 1, 0, P)
                if more:
                    pe.wait_ge(g_d, 3 * (u + 1) + 1)
                    pe.wait_ge(v_x, 5 * (u + 1) + 4)
                    spread_max(0)
                if prev:
                    pv(kp, 2)
                    pv(kp, 3)
                if more:
                    pe.wait_ge(g_d, 3 * (u + 1) + 3)
                    pe.wait_ge(v_x, 5 * (u + 1) + 5)
                    spread_max(1)

            pe.wait_ge(g_const, 4)
            pe.wait_ge(v_fold, 3)
            pe.wait_ge(v_xl, 1)
            project_q(0)
            project_k(0)
            step(-1, ROUND - 1, -1, first=True, prev=False)
            pe.wait_ge(v_logit, 1)
            pe.wait_ge(v_xl, B)
            for k in range(HEAD):
                step(k, k, 0, prev=k > 0)
            with pe.Fori(0, ROUNDS - 1) as r:
                for k in range(HEAD, HEAD + ROUND):
                    step(ROUND * r + k, k % ROUND, r if k < ROUND else r + 1)
            for k in range(HEAD, ROUND):
                step(UNITS - ROUND + k, k, ROUNDS - 1, more=k < ROUND - 1, far=k < ROUND - 2)
            tb = hbank + ebank
            pe.wait_ge(v_xhat, 3)
            for b in range(B):
                if b == 3:
                    pe.wait_ge(a_e, 6 * UNITS - 2)
                for j in range(TT):
                    last = nc.tensor.transpose(tb[b][:, j * P:(j + 1) * P], xhat[:, b * TT + j, :], ident[:])
                last.then_inc(p_xhatT, 1)
            pe.wait_ge(v_pick, 1)
            for b in range(B):
                pe.wait_ge(a_xhatT, b + 1)
                for j in range(TT):
                    last = nc.tensor.transpose(tb[b][0:E, j * P:(j + 1) * P], pick[:, b * TT + j, :], ident[:])
                last.then_inc(p_maskT, 1)

            def hidden(n):
                b, g = n // G, n % G
                if n >= 3:
                    pe.wait_ge(a_hid, n - 2)
                mm(hbank[n % 3][:], w1s[:].rearrange("p e h -> p (e h)")[:, g * P:(g + 1) * P],
                   xhatT[:, b * T:(b + 1) * T], start=True, stop=True).then_inc(p_hid, 1)

            for n in range(3):
                pe.wait_ge(v_maskT, n + 1)
                hidden(n)
            pe.wait_ge(g_s, 2 * UNITS)
            pe.wait_ge(v_r, UNITS - 1)
            denominators(1)
            pe.wait_ge(v_n, UNITS - 1)
            for j in range(TT):
                pv(ROUND - 1, j)

            def output_block(n):
                b, r = n // BLOCKS, n % BLOCKS
                dst = obank[b % 2][:]
                if r == 0:
                    if b == 1:
                        pe.wait_ge(v_r, UNITS)
                    if b >= 2:
                        pe.wait_ge(a_oT, b - 1)
                    for part in b2_parts:
                        mm(dst, part, maskT[:, b * T:(b + 1) * T], start=part is b2_parts[0], stop=False)
                if r < PAIRS:
                    wh, wl = (part[:, r * C:(r + 1) * C] for part in wout_parts)
                else:
                    wh, wl = (part[:, r - PAIRS, :] for part in w2_parts)
                high, low = RING[n % len(RING)]
                pe.wait_ge(a_hi, n + 1)
                mm(dst, wh, high, start=False, stop=False)
                mm(dst, wl, high, start=False, stop=False)
                if by_pool(n):
                    pe.wait_ge(g_lo, n // 4 + 1)
                else:
                    pe.wait_ge(v_lo, n + 1 - (n + 1) // 4)
                mm(dst, wh, low, start=False, stop=r == BLOCKS - 1).then_inc(s_used, 1)

            def output_rows(b):
                if b == 0:
                    pe.wait_ge(v_n, UNITS)
                if b >= 2:
                    pe.wait_ge(v_o, b - 1)
                for part, (pb, t0, t1, dst) in enumerate(PARTS):
                    if pb == b:
                        pe.wait_ge(a_oT, part + 1)
                        for j in range(t0, t1):
                            last = nc.tensor.transpose(dst[:, j * P:(j + 1) * P], outT[b % 2][:, j * P:(j + 1) * P],
                                                       ident[:])
                        last.then_inc(s_o, 1)

            pe.wait_ge(v_maskT, B)
            pe.wait_ge(v_w, 1)
            for n in range(EARLY):
                output_block(n)
            for n in range(G * B):
                b, g = n // G, n % G
                if n >= 3:
                    hidden(n)
                if n >= 2:
                    pe.wait_ge(v_gm, n - 1)
                mm(ebank[n % 2][:], expand[:, g * P:(g + 1) * P], maskT[:, b * T:(b + 1) * T],
                   start=True, stop=True).then_inc(p_exp, 1)
                output_block(n + EARLY)
            for n in range(G * B + EARLY, B * BLOCKS):
                output_block(n)
                if n % BLOCKS == 6 and n > BLOCKS:
                    output_rows(n // BLOCKS - 1)
            output_rows(B - 1)


_INS = ["L0_attn_x", "L0_attn_w_kv_down", "L0_attn_w_kv_up", "L0_attn_w_q", "L0_attn_w_out", "L0_ffn_Wg",
        "L0_ffn_ln_scale", "L0_ffn_ln_bias", "L0_ffn_W1", "L0_ffn_b1", "L0_ffn_W2", "L0_ffn_b2"]


def kernel(**inputs):
    import numpy as _np
    import concourse.bacc as _bacc
    from concourse import mybir as _mybir
    from concourse.bass_utils import run_bass_kernel_spmd as _run

    nc = _bacc.Bacc("TRN2", target_bir_lowering=False, num_devices=1)
    arrays, args = {}, []
    for name in _INS:
        a = _np.ascontiguousarray(inputs[name])
        arrays[f"in_{name}_dram"] = a
        args.append(nc.dram_tensor(f"in_{name}_dram", a.shape, _mybir.dt.from_np(a.dtype), kind="ExternalInput").ap())
    shape = inputs["L0_attn_x"].shape
    dt = _mybir.dt.from_np(_np.dtype("float32"))
    args.append(nc.dram_tensor("out_0_dram", shape, dt, kind="ExternalOutput").ap())
    attention_and_experts(nc, *args)
    r = _run(nc, [arrays], core_ids=[0])
    return r.results[0]["out_0_dram"]
```
